# Optimizing a Trainium2 kernel written in Bass

```python
import numpy as np
import jax
import jax.numpy as jnp

def _softmax(x, axis=-1):
    return jax.nn.softmax(x, axis=axis)

def _gelu(x):
    return jax.nn.gelu(x, approximate=True)

def _silu(x):
    return jax.nn.silu(x)

def _sigmoid(x):
    return jax.nn.sigmoid(x)

def _layernorm(x, axis=-1, eps=1e-05):
    m = jnp.mean(x, axis=axis, keepdims=True)
    v = jnp.var(x, axis=axis, keepdims=True)
    return (x - m) / jnp.sqrt(v + eps)

def _scatter_add(tgt, idx, src, axis=0):
    return tgt.at[idx].add(src)

def _segment_sum(src, seg, n):
    return jax.ops.segment_sum(src, seg, n)
kernel_name = 'mk_decoder_preln_d1_seqx_r8_f086fe'

def setup_inputs(seed: int=0):
    np.random.seed(seed)
    _w = jnp.asarray

    def _rec_inputs():
        import jax
        import jax.numpy as jnp
        _rk = jax.random.key(seed)
        x = -0.0005847 + 1 * jax.random.normal(jax.random.fold_in(_rk, 1), (64, 128, 128), jnp.float32)
        _lenS = 128 - jax.random.randint(jax.random.fold_in(_rk, 7), (64,), 0, max(1, 128 // 4) + 1, jnp.int32)
        _lenS2 = 77 - jax.random.randint(jax.random.fold_in(_rk, 8), (64,), 0, max(1, 77 // 4) + 1, jnp.int32)
        _ctx_1024P = jax.random.normal(jax.random.fold_in(_rk, 11), (64, 16, 128), jnp.float32)
        _ctx_1024c = jax.random.dirichlet(jax.random.fold_in(_rk, 511), 0.3 * jnp.ones((16,), jnp.float32), (64, 77))
        _ctx_1024t = jnp.einsum('bsk,bkd->bsd', _ctx_1024c, _ctx_1024P)
        _ctx_1024t = _ctx_1024t * jax.lax.rsqrt(jnp.mean(jnp.square(_ctx_1024t)) + 1e-12) * 0.953939
        ctx_1024 = 2.81802e-05 + 1.00001 * (_ctx_1024t + 0.3 * jax.random.normal(jax.random.fold_in(_rk, 611), (64, 77, 128), jnp.float32))
        _validS = jnp.arange(128)[None, :] < _lenS[:, None]
        _validS2 = jnp.arange(77)[None, :] < _lenS2[:, None]
        _causal = jnp.tril(jnp.ones((128, 128), dtype=bool))
        mask_BxS2_ik1 = jnp.where(jnp.broadcast_to(_validS2[:, :], (64, 77)), 1, 0).astype(jnp.int32)
        return (x, ctx_1024, mask_BxS2_ik1)
    x, ctx_1024, mask_BxS2_ik1 = _rec_inputs()

    def _L0_attn_setup():
        import jax, jax.numpy as jnp
        import numpy as np
        B, L, D_IN, D_OUT, H, WIN = (1, 256, 128, 128, 16, 64)
        D_H = D_OUT // H
        key = jax.random.key(seed)
        ks = jax.random.split(key, 5)
        s = 0.02
        return {'x': jax.random.normal(ks[0], (B, L, D_IN), dtype=jnp.float32), 'Wq': jax.random.normal(ks[1], (D_IN, D_OUT), dtype=jnp.float32) * s, 'Wk': jax.random.normal(ks[2], (D_IN, D_OUT), dtype=jnp.float32) * s, 'Wv': jax.random.normal(ks[3], (D_IN, D_OUT), dtype=jnp.float32) * s, 'Wo': jax.random.normal(ks[4], (D_OUT, D_IN), dtype=jnp.float32) * s}
    _L0_attn_all = _L0_attn_setup()
    _L0_attn_in = {k: v for k, v in _L0_attn_all.items() if k in ('Wq', 'Wk', 'Wv', 'Wo')}
    del _L0_attn_all

    def _L0_xattn_setup():
        import jax, jax.numpy as jnp
        import numpy as np
        DIM = 128
        NUM_HEADS = 16
        HEAD_DIM = DIM // NUM_HEADS
        SCALE = HEAD_DIM ** (-0.5)

        def _split_heads(x):
            B, L, _ = x.shape
            return x.reshape(B, L, NUM_HEADS, HEAD_DIM).transpose(0, 2, 1, 3)
        key = jax.random.key(seed)
        ks = jax.random.split(key, 12)
        B, Q, S = (4, 900, 512)
        inp = {'query_vectors': jax.random.normal(ks[0], (B, Q, DIM), jnp.float32), 'key_input_flatten': jax.random.normal(ks[1], (B, S, DIM), jnp.float32), 'value_input_flatten': jax.random.normal(ks[2], (B, S, DIM), jnp.float32), 'attention_mask': jax.random.randint(ks[3], (B, S), 0, 2, jnp.int32), 'Wq': jax.random.normal(ks[4], (DIM, DIM), jnp.float32) * 0.02, 'bq': jnp.zeros((DIM,), jnp.float32), 'Wk': jax.random.normal(ks[5], (DIM, DIM), jnp.float32) * 0.02, 'bk': jnp.zeros((DIM,), jnp.float32), 'Wv': jax.random.normal(ks[6], (DIM, DIM), jnp.float32) * 0.02, 'bv': jnp.zeros((DIM,), jnp.float32), 'Wo': jax.random.normal(ks[7], (DIM, DIM), jnp.float32) * 0.02, 'bo': jnp.zeros((DIM,), jnp.float32)}
        return inp
    _L0_xattn_all = _L0_xattn_setup()
    _L0_xattn_in = {k: v for k, v in _L0_xattn_all.items() if k in ('Wq', 'bq', 'Wk', 'bk', 'Wv', 'bv', 'Wo', 'bo')}
    del _L0_xattn_all

    def _L0_ffn_setup():
        import jax, jax.numpy as jnp
        import numpy as np
        DIM = 128

        def _reference_tuple_inner(x, W_r, W_k, W_v, mu_r, mu_k):
            B, T, C = x.shape
            x_prev = jnp.concatenate([jnp.zeros((B, 1, C), x.dtype), x[:, :-1, :]], axis=1)
            xr = mu_r * x + (1.0 - mu_r) * x_prev
            xk = mu_k * x + (1.0 - mu_k) * x_prev
            r = jax.nn.sigmoid(jnp.einsum('btc,dc->btd', xr, W_r))
            k = jnp.einsum('btc,dc->btd', xk, W_k)
            k_act = jnp.square(jax.nn.relu(k))
            out = r * jnp.einsum('btc,dc->btd', k_act, W_v)
            new_state = x[:, -1, :]
            return (out, new_state)
        key = jax.random.key(seed)
        ks = jax.random.split(key, 6)
        B, T, C = (8, 256, DIM)
        x = jax.random.normal(ks[0], (B, T, C), dtype=jnp.float32)
        s = 1.0 / np.sqrt(C)
        W_r = jax.random.uniform(ks[1], (C, C), jnp.float32, -s, s)
        W_k = jax.random.uniform(ks[2], (C, C), jnp.float32, -s, s)
        W_v = jax.random.uniform(ks[3], (C, C), jnp.float32, -s, s)
        mu_r = jax.random.uniform(ks[4], (C,), jnp.float32)
        mu_k = jax.random.uniform(ks[5], (C,), jnp.float32)
        return {'x': x, 'W_r': W_r, 'W_k': W_k, 'W_v': W_v, 'mu_r': mu_r, 'mu_k': mu_k}
    _L0_ffn_all = _L0_ffn_setup()
    _L0_ffn_in = {k: v for k, v in _L0_ffn_all.items() if k in ('W_r', 'W_k', 'W_v', 'mu_r', 'mu_k')}
    del _L0_ffn_all
    return {'x': x, 'ctx_1024': ctx_1024, 'mask_BxS2_ik1': mask_BxS2_ik1, 'L0_attn_Wq': _L0_attn_in['Wq'], 'L0_attn_Wk': _L0_attn_in['Wk'], 'L0_attn_Wv': _L0_attn_in['Wv'], 'L0_attn_Wo': _L0_attn_in['Wo'], 'L0_xattn_Wq': _L0_xattn_in['Wq'], 'L0_xattn_bq': _L0_xattn_in['bq'], 'L0_xattn_Wk': _L0_xattn_in['Wk'], 'L0_xattn_bk': _L0_xattn_in['bk'], 'L0_xattn_Wv': _L0_xattn_in['Wv'], 'L0_xattn_bv': _L0_xattn_in['bv'], 'L0_xattn_Wo': _L0_xattn_in['Wo'], 'L0_xattn_bo': _L0_xattn_in['bo'], 'L0_ffn_W_r': _L0_ffn_in['W_r'], 'L0_ffn_W_k': _L0_ffn_in['W_k'], 'L0_ffn_W_v': _L0_ffn_in['W_v'], 'L0_ffn_mu_r': _L0_ffn_in['mu_r'], 'L0_ffn_mu_k': _L0_ffn_in['mu_k']}

def reference(x, ctx_1024, mask_BxS2_ik1, L0_attn_Wq, L0_attn_Wk, L0_attn_Wv, L0_attn_Wo, L0_xattn_Wq, L0_xattn_bq, L0_xattn_Wk, L0_xattn_bk, L0_xattn_Wv, L0_xattn_bv, L0_xattn_Wo, L0_xattn_bo, L0_ffn_W_r, L0_ffn_W_k, L0_ffn_W_v, L0_ffn_mu_r, L0_ffn_mu_k):
    import jax
    import jax.numpy as jnp

    def _L0_attn_ref(x, Wq, Wk, Wv, Wo):
        import jax, jax.numpy as jnp
        import numpy as np
        B, L, D_IN, D_OUT, H, WIN = (1, 256, 128, 128, 16, 64)
        D_H = D_OUT // H
        Bx, Lx, _ = x.shape
        W = min(WIN, Lx)
        scale = D_H ** (-0.5)

        def split_heads(t):
            return t.reshape(Bx, Lx, H, D_H).transpose(0, 2, 1, 3)
        q = split_heads(x @ Wq)
        k = split_heads(x @ Wk)
        v = split_heads(x @ Wv)
        offsets = jnp.arange(W) - (W - 1)
        idx = jnp.arange(Lx)[:, None] + offsets[None, :]
        invalid = idx < 0
        idx = jnp.clip(idx, 0, Lx - 1)
        k_win = jnp.take(k, idx, axis=2)
        v_win = jnp.take(v, idx, axis=2)
        scores = jnp.einsum('bhld,bhlwd->bhlw', q, k_win) * scale
        scores = jnp.where(invalid[None, None, :, :], -jnp.inf, scores)
        attn = jax.nn.softmax(scores, axis=-1)
        ctx = jnp.einsum('bhlw,bhlwd->bhld', attn, v_win)
        ctx = ctx.transpose(0, 2, 1, 3).reshape(Bx, Lx, D_OUT)
        return ctx @ Wo

    def _L0_xattn_ref(query_vectors, key_input_flatten, value_input_flatten, attention_mask, Wq, bq, Wk, bk, Wv, bv, Wo, bo):
        import jax, jax.numpy as jnp
        import numpy as np
        DIM = 128
        NUM_HEADS = 16
        HEAD_DIM = DIM // NUM_HEADS
        SCALE = HEAD_DIM ** (-0.5)

        def _split_heads(x):
            B, L, _ = x.shape
            return x.reshape(B, L, NUM_HEADS, HEAD_DIM).transpose(0, 2, 1, 3)
        B, Q, D = query_vectors.shape
        q = _split_heads(query_vectors @ Wq.T + bq) * SCALE
        k = _split_heads(key_input_flatten @ Wk.T + bk)
        v = _split_heads(value_input_flatten @ Wv.T + bv)
        scores = jnp.einsum('bhqd,bhsd->bhqs', q, k)
        scores = scores + attention_mask.astype(scores.dtype)[:, None, None, :] * -100.0
        probs = jax.nn.softmax(scores, axis=-1)
        ctx = jnp.einsum('bhqs,bhsd->bhqd', probs, v)
        ctx = ctx.transpose(0, 2, 1, 3).reshape(B, Q, D)
        return ctx @ Wo.T + bo

    def _L0_ffn_ref(x, W_r, W_k, W_v, mu_r, mu_k):
        import jax, jax.numpy as jnp
        import numpy as np
        DIM = 128

        def _reference_tuple_inner(x, W_r, W_k, W_v, mu_r, mu_k):
            B, T, C = x.shape
            x_prev = jnp.concatenate([jnp.zeros((B, 1, C), x.dtype), x[:, :-1, :]], axis=1)
            xr = mu_r * x + (1.0 - mu_r) * x_prev
            xk = mu_k * x + (1.0 - mu_k) * x_prev
            r = jax.nn.sigmoid(jnp.einsum('btc,dc->btd', xr, W_r))
            k = jnp.einsum('btc,dc->btd', xk, W_k)
            k_act = jnp.square(jax.nn.relu(k))
            out = r * jnp.einsum('btc,dc->btd', k_act, W_v)
            new_state = x[:, -1, :]
            return (out, new_state)
        return _reference_tuple_inner(x, W_r, W_k, W_v, mu_r, mu_k)[0]
    x = x + _L0_attn_ref(_layernorm(x, axis=-1), L0_attn_Wq, L0_attn_Wk, L0_attn_Wv, L0_attn_Wo)
    x = x + _L0_xattn_ref(_layernorm(x, axis=-1), ctx_1024, ctx_1024, mask_BxS2_ik1, L0_xattn_Wq, L0_xattn_bq, L0_xattn_Wk, L0_xattn_bk, L0_xattn_Wv, L0_xattn_bv, L0_xattn_Wo, L0_xattn_bo)
    x = x + _L0_ffn_ref(_layernorm(x, axis=-1), L0_ffn_W_r, L0_ffn_W_k, L0_ffn_W_v, L0_ffn_mu_r, L0_ffn_mu_k)
    return x

_drawn_inputs = setup_inputs


def setup_inputs(seed=0):
    import zlib

    import numpy as np

    out = dict(_drawn_inputs(seed))
    spreads = {'L0_xattn_bq': (0.0, 0.8),
     'L0_xattn_bk': (0.0, 0.8),
     'L0_xattn_bv': (0.0, 0.343),
     'L0_xattn_bo': (0.0, 0.1)}
    factors = {'L0_attn_Wq': 8.0,
     'L0_attn_Wk': 8.0,
     'L0_attn_Wv': 5.227,
     'L0_attn_Wo': 5.173,
     'L0_xattn_Wq': 8.0,
     'L0_xattn_Wk': 8.0,
     'L0_ffn_W_r': 3.171,
     'L0_ffn_mu_r': 6.277}
    for name, (base, spread) in spreads.items():
        noise = np.random.default_rng([zlib.crc32(name.encode()), seed]).standard_normal(out[name].shape)
        drawn = base * np.exp(spread * noise) if base else spread * noise
        out[name] = jnp.asarray(drawn.astype(out[name].dtype))
    for name, factor in factors.items():
        out[name] = (out[name] * factor).astype(out[name].dtype)
    return out
```

```python
from contextlib import ExitStack

import concourse.bass as bass
from concourse import mybir

F32 = mybir.dt.float32
BF16 = mybir.dt.bfloat16
I32 = mybir.dt.int32
ALU = mybir.AluOpType
ACT = mybir.ActivationFunctionType
AX_X = mybir.AxisListType.X

P = 128
BATCH, T, D = 64, 128, 128
TC = 77
H, DH = 16, 8
G = H // 2
QB = 4
NQ = BATCH // QB
NT, NC = QB * T, QB * TC
WIN = 64
HALF = T // 2
SCALE = float(DH) ** -0.5
EPS = 1e-5
MASKED = -1e30
MASK_WEIGHT = -100.0

QPART = (0, 1, 2, 0, 1, 0)
KPART = (0, 0, 0, 1, 1, 2)
NSTACK = 2 * len(QPART) * DH
SHIFT_SELF = NSTACK
BIAS_CROSS = NSTACK
SHIFT_CROSS = NSTACK + 3


def decoder_layer(nc, x, ctx, mask, wq, wk, wv, wo, cwq, cbq, cwk, cbk, cwv, cbv, cwo, cbo,
                  fwr, fwk, fwv, mu_r, mu_k, out):
    x_quads = x.rearrange("(n b) t d -> n t b d", b=QB)
    out_quads = out.rearrange("(n b) t d -> n t b d", b=QB)
    ctx_quads = ctx.rearrange("(n b) s d -> n s b d", b=QB)

    def scratch(name, shape):
        return nc.dram_tensor(name, shape, BF16).ap()

    q_scr = scratch("q_scr", [2, 3, DH, G, NT])
    k_scr = scratch("k_scr", [2, 3, DH, G, NT])
    cq_scr = scratch("cq_scr", [2, 3, DH, G, NT])
    ck_scr = scratch("ck_scr", [2, 3, DH, G, NC])
    bias_scr = scratch("bias_scr", [3, NQ, G, NC])

    with ExitStack() as stack:
        def sb(name, shape, dt=F32):
            return stack.enter_context(nc.sbuf_tensor(name, shape, dt))

        def sem(name):
            return stack.enter_context(nc.semaphore(name))

        ident = sb("ident", [P, P])
        ident_bf = sb("ident_bf", [P, 4, P], BF16)
        band = sb("band", [P, 4, P], BF16)
        band_lo = sb("band_lo", [P, G, HALF], BF16)
        pick_hi = sb("pick_hi", [P, 2, HALF], BF16)
        pick_lo = sb("pick_lo", [P, 2, HALF], BF16)
        head_ones = sb("head_ones", [P, 4, 32])
        one = sb("one", [P, P])
        neg_half = sb("neg_half", [P, QB])
        w_raw = sb("w_raw", [P, 11, P])
        wT = sb("wT", [P, 11, P])
        (SQ, SK, SV, SO, CQ, CK, CV, CO, FR, FK, FV) = range(11)
        bias_rows = sb("bias_rows", [1, 3, P])
        bias_perm = sb("bias_perm", [1, 3, P])
        bias_cols = sb("bias_cols", [P, 3])
        cbv_wide = sb("cbv_wide", [P, P])
        cbo_wide = sb("cbo_wide", [P, P])
        out_bias = sb("out_bias", [P, P])
        mu = sb("mu", [P, 2])
        mu_rest = sb("mu_rest", [P, 2])
        mask_in = sb("mask_in", [NQ, NC], I32)
        mask_f = sb("mask_f", [NQ, NC])
        mask_r = sb("mask_r", [NQ, NC])
        mask_parts = sb("mask_parts", [NQ, 3, NC], BF16)

        x_in = sb("x_in", [P, QB, D])
        stats = [sb(f"stats{n}", [P, QB, 6]) for n in range(3)]
        moments = [sb(f"moments{n}", [P, 6, QB]) for n in range(3)]
        var_eps = [sb(f"var_eps{n}", [P, QB]) for n in range(3)]
        rstd = [sb(f"rstd{n}", [P, QB]) for n in range(3)]
        xn = [sb(f"xn{n}", [P, QB, D]) for n in range(3)]
        xnT = sb("xnT", [P, NT])
        q_parts = sb("q_parts", [P, 3, NT], BF16)
        k_parts = sb("k_parts", [P, 3, NT], BF16)
        q_rest = sb("q_rest", [P, NT])
        k_rest = sb("k_rest", [P, NT])
        q_stack = sb("q_stack", [P, 2, G, QB, T], BF16)
        k_stack = sb("k_stack", [P, G, QB, T], BF16)
        v_heads = sb("v_heads", [P, QB, H, 32])
        neg_max = sb("neg_max", [P, 4, G, QB])
        max_f = sb("max_f", [G * QB, 2, T])
        max_hi = sb("max_hi", [G * QB, 2, T], BF16)
        max_mid = sb("max_mid", [G * QB, 2, T], BF16)
        probs = sb("probs", [P, 2, 4, 2, T])
        den_inv = sb("den_inv", [P, 2, T])
        attT = sb("attT", [P, QB, T])
        x1 = sb("x1", [P, QB, D])
        x1b = sb("x1b", [P, QB, D])

        ctx_in = sb("ctx_in", [TC, QB, D])
        ctxT = sb("ctxT", [P, NC])
        xcT = sb("xcT", [P, NT])
        cq_parts = sb("cq_parts", [P, 3, NT], BF16)
        ck_parts = sb("ck_parts", [P, 3, NC], BF16)
        cq_rest = sb("cq_rest", [P, NT])
        ck_rest = sb("ck_rest", [P, NC])
        cq_stack = sb("cq_stack", [P, 2, G, QB, T], BF16)
        ck_stack = sb("ck_stack", [P, G, QB, TC], BF16)
        cv_heads = sb("cv_heads", [P, QB, H, 32])
        cneg_max = sb("cneg_max", [P, 4, G, QB])
        cmax_f = sb("cmax_f", [2 * G * QB, T])
        cmax_hi = sb("cmax_hi", [2 * G * QB, T], BF16)
        cmax_mid = sb("cmax_mid", [2 * G * QB, T], BF16)
        cprobs = sb("cprobs", [P, 2, 4, 2, T])
        cden_inv = sb("cden_inv", [P, 2, T])
        cattT = sb("cattT", [P, QB, T])
        x2 = sb("x2", [P, QB, D])
        xeT = sb("xeT", [P, QB, T + 1])
        mix_a = sb("mix_a", [P, 2, QB, T])
        mixed = sb("mixed", [P, 2, QB, T])
        k_relu = sb("k_relu", [P, NT])
        k_act = sb("k_act", [P, QB, T])
        gate_e = sb("gate_e", [P, NT])
        gate_d = sb("gate_d", [P, NT])
        gate = sb("gate", [P, NT])
        y_gated = sb("y_gated", [P, NT])
        y_out = sb("y_out", [P, QB, D])

        score = [stack.enter_context(nc.psum_tensor(f"score{n}", [P, 1024], F32)) for n in range(2)]
        sums = [stack.enter_context(nc.psum_tensor(f"sums{n}", [P, 4, T], F32)) for n in range(2)]
        proj = [stack.enter_context(nc.psum_tensor(f"proj{n}", [P, 512], F32)) for n in range(2)]

        w_in = sem("w_in")
        small_in = sem("small_in")
        mask_loaded = sem("mask_loaded")
        ident_zero = sem("ident_zero")
        ident_made = sem("ident_made")
        consts_made = sem("consts_made")
        zeros_made = sem("zeros_made")
        ones_rows = sem("ones_rows")
        w_turned = sem("w_turned")
        w_ready = sem("w_ready")
        bias_permuted = sem("bias_permuted")
        bias_turned = sem("bias_turned")
        bias_ready = sem("bias_ready")
        bias_wide = sem("bias_wide")
        out_bias_mm = sem("out_bias_mm")
        setup_dve = sem("setup_dve")
        bias_stored = sem("bias_stored")

        x_loaded = sem("x_loaded")
        ln_stats = [sem(f"ln_stats{n}") for n in range(3)]
        ln_moments = [sem(f"ln_moments{n}") for n in range(3)]
        ln_rstd = [sem(f"ln_rstd{n}") for n in range(3)]
        ln_out = [sem(f"ln_out{n}") for n in range(3)]
        xnT_made = sem("xnT_made")
        xnT_ready = sem("xnT_ready")
        q_made = sem("q_made")
        q_hi = sem("q_hi")
        q_left = sem("q_left")
        q_mid = sem("q_mid")
        q_lo = sem("q_lo")
        k_made = sem("k_made")
        k_hi = sem("k_hi")
        k_left = sem("k_left")
        k_mid = sem("k_mid")
        k_lo = sem("k_lo")
        v_made = sem("v_made")
        v_ready = sem("v_ready")
        q_stored = sem("q_stored")
        k_stored = sem("k_stored")
        q_stacked = sem("q_stacked")
        k_stacked = sem("k_stacked")
        s_made = sem("s_made")
        max_taken = sem("max_taken")
        maxT_made = sem("maxT_made")
        max_f_ready = sem("max_f_ready")
        max_hi_ready = sem("max_hi_ready")
        max_mid_ready = sem("max_mid_ready")
        shift_in = sem("shift_in")
        sT_made = sem("sT_made")
        exp_done = sem("exp_done")
        pv_done = sem("pv_done")
        den_ready = sem("den_ready")
        att_ready = sem("att_ready")
        o_made = sem("o_made")
        x1_ready = sem("x1_ready")
        x1b_ready = sem("x1b_ready")

        ctx_loaded = sem("ctx_loaded")
        ctxT_made = sem("ctxT_made")
        ctxT_ready = sem("ctxT_ready")
        cbias_in = sem("cbias_in")
        xcT_made = sem("xcT_made")
        xcT_ready = sem("xcT_ready")
        cq_made = sem("cq_made")
        cq_hi = sem("cq_hi")
        cq_left = sem("cq_left")
        cq_mid = sem("cq_mid")
        cq_lo = sem("cq_lo")
        ck_made = sem("ck_made")
        ck_hi = sem("ck_hi")
        ck_left = sem("ck_left")
        ck_mid = sem("ck_mid")
        ck_lo = sem("ck_lo")
        cv_made = sem("cv_made")
        cv_ready = sem("cv_ready")
        cq_stored = sem("cq_stored")
        ck_stored = sem("ck_stored")
        cq_stacked = sem("cq_stacked")
        ck_stacked = sem("ck_stacked")
        cs_made = sem("cs_made")
        cmax_taken = sem("cmax_taken")
        cmaxT_made = sem("cmaxT_made")
        cmax_f_ready = sem("cmax_f_ready")
        cmax_hi_ready = sem("cmax_hi_ready")
        cmax_mid_ready = sem("cmax_mid_ready")
        cshift_in = sem("cshift_in")
        csT_made = sem("csT_made")
        cexp_done = sem("cexp_done")
        cpv_done = sem("cpv_done")
        cden_ready = sem("cden_ready")
        catt_ready = sem("catt_ready")
        co_made = sem("co_made")
        x2_ready = sem("x2_ready")
        xeT_made = sem("xeT_made")
        xeT_ready = sem("xeT_ready")
        mix_part = sem("mix_part")
        mix_ready = sem("mix_ready")
        fk_made = sem("fk_made")
        relu_ready = sem("relu_ready")
        k_act_ready = sem("k_act_ready")
        fr_made = sem("fr_made")
        gate_e_ready = sem("gate_e_ready")
        gate_d_ready = sem("gate_d_ready")
        gate_ready = sem("gate_ready")
        fv_made = sem("fv_made")
        y_gated_ready = sem("y_gated_ready")
        y_ready = sem("y_ready")
        y_stored = sem("y_stored")

        block = stack.enter_context(nc.Block())

        def schedule(eng, step):
            step(0, True, False)
            step(1, True, True)
            with eng.Fori(2, NQ) as t:
                step(t, True, True)
            step(NQ, False, True)

        @block.sync
        def _(sp):
            for n, w in enumerate((wq, wk, wv, wo, cwq, cwk, cwv, cwo, fwr, fwk, fwv)):
                sp.dma_start(w_raw[:, n, :], w).then_inc(w_in, 16)
            for n, b in enumerate((cbq, cbk, cbv)):
                sp.dma_start(bias_rows[:, n, :], b.rearrange("(o d) -> o d", o=1)).then_inc(small_in, 16)
            for n, m in enumerate((mu_r, mu_k)):
                sp.dma_start(mu[:, n:n + 1], m.rearrange("(d o) -> d o", o=1)).then_inc(small_in, 16)
            sp.dma_start(cbo_wide[:, :], cbo.partition_broadcast(P)).then_inc(small_in, 16)
            sp.dma_start(mask_in[:, :], mask.rearrange("(n b) s -> n (b s)", b=QB)).then_inc(mask_loaded, 16)
            sp.wait_ge(zeros_made, 4)
            for r in range(4):
                sp.dma_start(cq_stack[BIAS_CROSS:BIAS_CROSS + 3, r // 2, 4 * (r % 2):4 * (r % 2) + 4]
                             .rearrange("p g b q -> p (g b q)"),
                             ck_stack[BIAS_CROSS:BIAS_CROSS + 3]
                             .rearrange("p g b k -> p (g b k)")[:, 0:2048]).then_inc(ones_rows, 16)
            sp.wait_ge(setup_dve, 10)
            for g in range(G):
                sp.dma_start(bias_scr[:, :, g, :].rearrange("c n s -> n c s"), mask_parts[:, :, :])\
                    .then_inc(bias_stored, 16)

            def store_parts(parts, scr, stored):
                for a in range(2):
                    sp.dma_start(scr[a].rearrange("p d g t -> (d g) p t"),
                                 parts[HALF * a:HALF * a + HALF]).then_inc(stored, 16)

            def stack_queries(scr, dst, stacked):
                rows = dst.rearrange("p a g b q -> p a (g b q)")
                for a in range(2):
                    for c, n in ((0, 3), (3, 2), (5, 1)):
                        r = 48 * a + DH * c
                        sp.dma_start(rows[r:r + DH * n, a, :],
                                     scr[a, 0:n].rearrange("p d g t -> (p d) (g t)")).then_inc(stacked, 16)

            def stack_keys(scr, dst, stacked):
                rows = dst.rearrange("p g b k -> p (g b k)")
                for a in range(2):
                    for c, part in enumerate(KPART):
                        r = 48 * a + DH * c
                        sp.dma_start(rows[r:r + DH, :],
                                     scr[a, part].rearrange("d g t -> d (g t)")).then_inc(stacked, 16)

            def step(t, front, back):
                u = t - 1
                if front:
                    if back:
                        sp.wait_ge(x1_ready, u + 1)
                    sp.dma_start(x_in[:, :, :], x_quads[t]).then_inc(x_loaded, 16)
                    if back:
                        sp.wait_ge(ctxT_made, u + 1)
                    sp.dma_start(ctx_in[:, :, :], ctx_quads[t]).then_inc(ctx_loaded, 16)
                    sp.wait_ge(q_lo, t + 1)
                    store_parts(q_parts[:, :, :], q_scr, q_stored)
                    sp.wait_ge(k_lo, t + 1)
                    store_parts(k_parts[:, :, :], k_scr, k_stored)
                    if back:
                        sp.wait_ge(sT_made, 8 * u + 8)
                    else:
                        sp.wait_ge(zeros_made, 4)
                    sp.wait_ge(q_stored, 32 * t + 32)
                    stack_queries(q_scr, q_stack[:, :, :, :, :], q_stacked)
                    sp.wait_ge(k_stored, 32 * t + 32)
                    stack_keys(k_scr, k_stack[:, :, :, :], k_stacked)
                if back:
                    sp.wait_ge(cmax_mid_ready, u + 1)
                    sp.wait_ge(cmax_hi_ready, u + 1)
                    for a in range(2):
                        for part, src in enumerate((cmax_hi, cmax_mid)):
                            r = SHIFT_CROSS + 2 * a + part
                            sp.dma_start(cq_stack[r:r + 1, a].rearrange("o g b q -> o (g b) q"),
                                         src[32 * a:32 * a + 32, :]).then_inc(cshift_in, 16)
                if front:
                    sp.wait_ge(max_mid_ready, t + 1)
                    sp.wait_ge(max_hi_ready, t + 1)
                    for a in range(2):
                        for part, src in enumerate((max_hi, max_mid)):
                            r = SHIFT_SELF + 2 * a + part
                            sp.dma_start(q_stack[r:r + 1, a].rearrange("o g b q -> o (g b) q"),
                                         src[:, a, :]).then_inc(shift_in, 16)
                    sp.wait_ge(ck_lo, t + 1)
                    store_parts(ck_parts[:, :, :], ck_scr, ck_stored)
                    sp.wait_ge(ck_stored, 32 * t + 32)
                    if back:
                        sp.wait_ge(csT_made, 8 * u + 8)
                    else:
                        sp.wait_ge(ones_rows, 64)
                        sp.wait_ge(bias_stored, 16 * G)
                    stack_keys(ck_scr, ck_stack[:, :, :, :], ck_stacked)
                    sp.dma_start(ck_stack[BIAS_CROSS:BIAS_CROSS + 3].rearrange("p g b k -> p (g b k)"),
                                 bias_scr[:, t].rearrange("c g s -> c (g s)")).then_inc(cbias_in, 16)
                if back:
                    sp.wait_ge(y_ready, u + 1)
                    sp.dma_start(out_quads[u], y_out[:, :, :]).then_inc(y_stored, 16)
                if front:
                    sp.wait_ge(cq_lo, t + 1)
                    store_parts(cq_parts[:, :, :], cq_scr, cq_stored)
                    sp.wait_ge(cq_stored, 32 * t + 32)
                    stack_queries(cq_scr, cq_stack[:, :, :, :, :], cq_stacked)

            schedule(sp, step)
            sp.wait_ge(y_stored, 16 * NQ)

        @block.gpsimd
        def _(pool):
            nc.gpsimd.memset(ident[:, :], 0.0).then_inc(ident_zero, 1)
            nc.gpsimd.memset(band[:, :, :], 0.0).then_inc(ident_zero, 1)
            pool.wait_ge(ident_zero, 2)
            nc.gpsimd.affine_select(out=ident[:, :], in_=ident[:, :], compare_op=ALU.not_equal, fill=1.0,
                                    base=0, pattern=[[-1, P]], channel_multiplier=1).then_inc(ident_made, 1)
            nc.gpsimd.affine_select(out=band[:, :, :], in_=band[:, :, :], compare_op=ALU.is_ge, fill=MASKED,
                                    base=0, pattern=[[0, 4], [-1, P]], channel_multiplier=1)\
                .then_inc(ident_made, 1)
            pool.wait_ge(ident_made, 2)
            nc.gpsimd.affine_select(out=band[:, :, :], in_=band[:, :, :], compare_op=ALU.is_ge, fill=MASKED,
                                    base=WIN - 1, pattern=[[0, 4], [1, P]], channel_multiplier=-1)\
                .then_inc(ident_made, 1)

            def rstd_of(n, q):
                pool.wait_ge(ln_moments[n], 7 * q + 7)
                pool.wait_ge(ln_out[n], QB * q)
                nc.gpsimd.tensor_tensor(rstd[n][:, :], var_eps[n][:, :], neg_half[:, :], ALU.pow)\
                    .then_inc(ln_rstd[n], 1)

            def low_part(parts, rest, left, mid, lo, stored, q):
                pool.wait_ge(left, q + 1)
                pool.wait_ge(mid, q + 1)
                nc.gpsimd.tensor_tensor(parts[:, 2, :], rest[:, :], parts[:, 1, :], ALU.subtract)\
                    .then_inc(lo, 1)

            def step(t, front, back):
                u = t - 1
                if front:
                    rstd_of(0, t)
                    if back:
                        pool.wait_ge(q_stored, 32 * u + 32)
                    low_part(q_parts, q_rest, q_left, q_mid, q_lo, q_stored, t)
                    if back:
                        pool.wait_ge(k_stored, 32 * u + 32)
                    low_part(k_parts, k_rest, k_left, k_mid, k_lo, k_stored, t)
                if back:
                    rstd_of(2, u)
                if front:
                    if back:
                        pool.wait_ge(ck_stored, 32 * u + 32)
                    low_part(ck_parts, ck_rest, ck_left, ck_mid, ck_lo, ck_stored, t)
                if back:
                    pool.wait_ge(relu_ready, u + 1)
                    pool.wait_ge(fv_made, u)
                    nc.gpsimd.tensor_tensor(k_act[:, :, :], k_relu[:, :].rearrange("p (b t) -> p b t", b=QB),
                                            k_relu[:, :].rearrange("p (b t) -> p b t", b=QB), ALU.mult)\
                        .then_inc(k_act_ready, 1)
                    pool.wait_ge(y_gated_ready, u + 1)
                    pool.wait_ge(y_stored, 16 * u)
                    nc.gpsimd.tensor_tensor(y_out[:, :, :], y_gated[:, :].rearrange("p (b d) -> p b d", b=QB),
                                            x2[:, :, :], ALU.add).then_inc(y_ready, 1)
                if front:
                    pool.wait_ge(x1_ready, t + 1)
                    if back:
                        pool.wait_ge(x2_ready, u + 1)
                    nc.gpsimd.tensor_tensor(x1b[:, :, :], x1[:, :, :],
                                            out_bias[:, :].unsqueeze(1).to_broadcast([P, QB, D]), ALU.add)\
                        .then_inc(x1b_ready, 1)
                    rstd_of(1, t)
                    if back:
                        pool.wait_ge(cq_stored, 32 * u + 32)
                    low_part(cq_parts, cq_rest, cq_left, cq_mid, cq_lo, cq_stored, t)

            pool.wait_ge(setup_dve, 8)
            schedule(pool, step)

        @block.scalar
        def _(act):
            act.wait_ge(w_turned, 2)
            for n in (CQ, CK, CV, CO, FR, FK, FV):
                src = proj[(n - CQ) // 4][:, P * ((n - CQ) % 4):P * ((n - CQ) % 4) + P]
                if n in (CQ, CK):
                    nc.scalar.activation(wT[:, n, :].rearrange("p (a d g) -> p a d g", a=2, d=DH),
                                         src.rearrange("p (g a d) -> p a d g", a=2, d=DH), ACT.Copy,
                                         scale=SCALE if n == CQ else 1.0).then_inc(w_ready, 1)
                else:
                    nc.scalar.activation(wT[:, n, :], src, ACT.Copy).then_inc(w_ready, 1)

            def step(t, front, back):
                u = t - 1
                if front:
                    act.wait_ge(xnT_made, t + 1)
                    if back:
                        act.wait_ge(v_made, u + 1)
                    nc.scalar.activation(xnT[:, :], proj[0][:, :], ACT.Copy).then_inc(xnT_ready, 1)
                    act.wait_ge(q_made, t + 1)
                    if back:
                        act.wait_ge(q_stored, 32 * u + 32)
                    nc.scalar.activation(q_parts[:, 0, :], proj[1][:, :], ACT.Copy).then_inc(q_hi, 1)
                    act.wait_ge(k_made, t + 1)
                    if back:
                        act.wait_ge(k_stored, 32 * u + 32)
                    nc.scalar.activation(k_parts[:, 0, :], proj[0][:, :], ACT.Copy).then_inc(k_hi, 1)
                    act.wait_ge(q_left, t + 1)
                    nc.scalar.activation(q_parts[:, 1, :], q_rest[:, :], ACT.Copy).then_inc(q_mid, 1)
                    act.wait_ge(k_left, t + 1)
                    nc.scalar.activation(k_parts[:, 1, :], k_rest[:, :], ACT.Copy).then_inc(k_mid, 1)
                if back:
                    act.wait_ge(cmaxT_made, u + 1)
                    act.wait_ge(cmax_mid_ready, u)
                    act.wait_ge(cshift_in, 64 * u)
                    nc.scalar.activation(cmax_f[:, :], proj[0][0:2 * G * QB, 0:T], ACT.Copy)\
                        .then_inc(cmax_f_ready, 1)
                    act.wait_ge(cmax_f_ready, u + 1)
                    nc.scalar.activation(cmax_hi[:, :], cmax_f[:, :], ACT.Copy).then_inc(cmax_hi_ready, 1)

                def exp_cross(k):
                    act.wait_ge(csT_made, 8 * u + k + 1)
                    act.wait_ge(cpv_done, 8 * u + max(k - 1, 0))
                    nc.scalar.activation(cprobs[0:TC, k % 2].rearrange("p g a q -> p (g a q)"),
                                         score[k % 2][0:TC, :], ACT.Exp).then_inc(cexp_done, 1)

                if back:
                    exp_cross(0)
                if front:
                    act.wait_ge(maxT_made, t + 1)
                    if back:
                        act.wait_ge(max_mid_ready, u + 1)
                        act.wait_ge(shift_in, 64 * u + 64)
                    for s in range(2):
                        nc.scalar.activation(max_f[:, :, HALF * s:HALF * s + HALF],
                                             proj[1][32 * s:32 * s + 32, 0:T]
                                             .rearrange("p (a q) -> p a q", a=2), ACT.Copy)\
                            .then_inc(max_f_ready, 1)
                    act.wait_ge(max_f_ready, 2 * t + 2)
                    nc.scalar.activation(max_hi[:, :, :], max_f[:, :, :], ACT.Copy).then_inc(max_hi_ready, 1)
                if back:
                    for k in range(1, 8):
                        exp_cross(k)
                if front:
                    act.wait_ge(ctxT_made, t + 1)
                    if back:
                        act.wait_ge(cv_made, u + 1)
                    else:
                        act.wait_ge(bias_ready, 3)
                    nc.scalar.activation(ctxT[:, :], proj[1][:, 0:NC], ACT.Copy).then_inc(ctxT_ready, 1)
                    act.wait_ge(ck_made, t + 1)
                    if back:
                        act.wait_ge(ck_stored, 32 * u + 32)
                    nc.scalar.activation(ck_parts[:, 0, :], proj[0][:, 0:NC], ACT.Identity,
                                         bias=bias_cols[:, 1:2]).then_inc(ck_hi, 1)
                    act.wait_ge(ck_left, t + 1)
                    nc.scalar.activation(ck_parts[:, 1, :], ck_rest[:, :], ACT.Copy).then_inc(ck_mid, 1)
                if back:
                    act.wait_ge(xeT_made, u + 1)
                    act.wait_ge(zeros_made, 4)
                    act.wait_ge(mix_ready, 2 * u)
                    nc.scalar.activation(xeT[:, :, 1:T + 1], proj[0][:, :].rearrange("p (b t) -> p b t", b=QB),
                                         ACT.Copy).then_inc(xeT_ready, 1)
                    act.wait_ge(fk_made, u + 1)
                    act.wait_ge(k_act_ready, u)
                    nc.scalar.activation(k_relu[:, :], proj[1][:, :], ACT.Relu).then_inc(relu_ready, 1)
                    act.wait_ge(fr_made, u + 1)
                    act.wait_ge(gate_d_ready, u)
                    nc.scalar.activation(gate_e[:, :], proj[0][:, :], ACT.Exp, scale=-1.0)\
                        .then_inc(gate_e_ready, 1)
                if front:
                    for k in range(8):
                        act.wait_ge(sT_made, 8 * t + k + 1)
                        if k >= 2 or back:
                            act.wait_ge(pv_done, 8 * t + k - 1)
                        nc.scalar.activation(probs[:, k % 2].rearrange("p g a q -> p (g a q)"),
                                             score[k % 2][:, :], ACT.Exp).then_inc(exp_done, 1)
                    act.wait_ge(xcT_made, t + 1)
                    if back:
                        act.wait_ge(cq_made, u + 1)
                    nc.scalar.activation(xcT[:, :], proj[1][:, :], ACT.Copy).then_inc(xcT_ready, 1)
                    act.wait_ge(cq_made, t + 1)
                    if back:
                        act.wait_ge(cq_stored, 32 * u + 32)
                    nc.scalar.activation(cq_parts[:, 0, :], proj[0][:, :], ACT.Identity,
                                         bias=bias_cols[:, 0:1]).then_inc(cq_hi, 1)
                    act.wait_ge(cq_left, t + 1)
                    nc.scalar.activation(cq_parts[:, 1, :], cq_rest[:, :], ACT.Copy).then_inc(cq_mid, 1)

            schedule(act, step)

        @block.vector
        def _(dve):
            nc.vector.memset(q_stack[:, :, :, :, :], 0.0).then_inc(zeros_made, 1)
            nc.vector.memset(cq_stack[:, :, :, :, :], 0.0).then_inc(zeros_made, 1)
            nc.vector.memset(k_stack[:, :, :, :], 1.0).then_inc(zeros_made, 1)
            nc.vector.memset(ck_stack[:, :, :, :], 1.0).then_inc(zeros_made, 1)
            nc.vector.memset(v_heads[:, :, :, :], 0.0).then_inc(consts_made, 1)
            nc.vector.memset(cv_heads[:, :, :, :], 0.0).then_inc(consts_made, 1)
            nc.vector.memset(cprobs[:, :, :, :, :], 0.0).then_inc(consts_made, 1)
            nc.vector.memset(xeT[:, :, :], 0.0).then_inc(consts_made, 1)
            nc.vector.memset(head_ones[:, :, :], 0.0).then_inc(consts_made, 1)
            nc.vector.memset(one[:, :], 1.0).then_inc(consts_made, 1)
            nc.vector.memset(neg_half[:, :], -0.5).then_inc(consts_made, 1)
            nc.vector.memset(neg_max[:, :, :, :], 0.0).then_inc(consts_made, 1)
            nc.vector.memset(cneg_max[:, :, :, :], 0.0).then_inc(consts_made, 1)
            dve.wait_ge(consts_made, 9)
            for i in range(4):
                nc.vector.memset(head_ones[:, i, DH * i:DH * i + DH], 1.0).then_inc(consts_made, 1)
            dve.wait_ge(ident_made, 3)
            for i in range(4):
                nc.vector.tensor_copy(ident_bf[:, i, :], ident[:, :]).then_inc(consts_made, 1)
            for s in range(2):
                nc.vector.tensor_copy(pick_lo[:, s, :], ident[:, 0:HALF]).then_inc(consts_made, 1)
                nc.vector.tensor_copy(pick_hi[:, s, :], ident[:, HALF:P]).then_inc(consts_made, 1)
            for s in range(2):
                nc.vector.tensor_copy(band_lo[:, 4 * s:4 * s + 4, :], band[:, :, 0:HALF]).then_inc(consts_made, 1)
            dve.wait_ge(w_in, 176)
            nc.vector.tensor_scalar(wT[:, SQ, :].rearrange("p (a d g) -> p a d g", a=2, d=DH),
                                    w_raw[:, SQ, :].rearrange("p (g a d) -> p a d g", a=2, d=DH),
                                    SCALE, None, ALU.mult).then_inc(w_ready, 1)
            nc.vector.tensor_copy(wT[:, SK, :].rearrange("p (a d g) -> p a d g", a=2, d=DH),
                                  w_raw[:, SK, :].rearrange("p (g a d) -> p a d g", a=2, d=DH)).then_inc(w_ready, 1)
            nc.vector.tensor_copy(wT[:, SV, :], w_raw[:, SV, :]).then_inc(w_ready, 1)
            nc.vector.tensor_copy(wT[:, SO, :], w_raw[:, SO, :]).then_inc(w_ready, 1)
            dve.wait_ge(small_in, 96)
            nc.vector.tensor_scalar(bias_perm[:, 0, :].rearrange("p (a d g) -> p a d g", a=2, d=DH),
                                    bias_rows[:, 0, :].rearrange("p (g a d) -> p a d g", a=2, d=DH),
                                    SCALE, None, ALU.mult).then_inc(bias_permuted, 1)
            nc.vector.tensor_copy(bias_perm[:, 1, :].rearrange("p (a d g) -> p a d g", a=2, d=DH),
                                  bias_rows[:, 1, :].rearrange("p (g a d) -> p a d g", a=2, d=DH))\
                .then_inc(bias_permuted, 1)
            nc.vector.tensor_copy(bias_perm[:, 2, :], bias_rows[:, 2, :]).then_inc(bias_permuted, 1)
            nc.vector.tensor_scalar(mu_rest[:, :], mu[:, :], -1.0, 1.0, ALU.mult, ALU.add).then_inc(setup_dve, 1)
            dve.wait_ge(bias_turned, 3)
            nc.vector.tensor_copy(bias_cols[:, :], score[0][:, 0:3]).then_inc(bias_ready, 3)
            dve.wait_ge(bias_ready, 3)
            nc.vector.tensor_scalar(cbv_wide[:, :], one[:, :], bias_cols[:, 2:3], None, ALU.mult)\
                .then_inc(bias_wide, 1)
            dve.wait_ge(out_bias_mm, 1)
            nc.vector.tensor_tensor(out_bias[:, :], score[0][:, 0:P], cbo_wide[:, :], ALU.add).then_inc(setup_dve, 7)
            dve.wait_ge(mask_loaded, 16)
            nc.vector.tensor_scalar(mask_f[:, :], mask_in[:, :], MASK_WEIGHT, None, ALU.mult)\
                .then_inc(bias_permuted, 1)
            dve.wait_ge(bias_permuted, 4)
            nc.vector.tensor_copy(mask_parts[:, 0, :], mask_f[:, :]).then_inc(bias_permuted, 1)
            dve.wait_ge(bias_permuted, 5)
            nc.vector.tensor_tensor(mask_r[:, :], mask_f[:, :], mask_parts[:, 0, :], ALU.subtract)\
                .then_inc(bias_permuted, 1)
            dve.wait_ge(bias_permuted, 6)
            nc.vector.tensor_copy(mask_parts[:, 1, :], mask_r[:, :]).then_inc(setup_dve, 1)
            dve.wait_ge(setup_dve, 9)
            nc.vector.tensor_tensor(mask_parts[:, 2, :], mask_r[:, :], mask_parts[:, 1, :], ALU.subtract)\
                .then_inc(setup_dve, 1)
            dve.wait_ge(setup_dve, 10)

            def layer_norm(n, src, q, used, used_value):
                first = isinstance(q, int) and q == 0
                for b in range(QB):
                    nc.vector.bn_stats(stats[n][:, b, :], src[:, b, :]).then_inc(ln_stats[n], 1)
                dve.wait_ge(ln_stats[n], QB * q + QB)
                dve.wait_ge(ln_rstd[n], q)
                mo, st = moments[n], stats[n]
                nc.vector.tensor_tensor(mo[:, 0], st[:, :, 1], st[:, :, 4], ALU.add).then_inc(ln_moments[n], 1)
                nc.vector.tensor_tensor(mo[:, 1], st[:, :, 1], st[:, :, 4], ALU.subtract).then_inc(ln_moments[n], 1)
                nc.vector.tensor_tensor(mo[:, 2], st[:, :, 2], st[:, :, 5], ALU.add).then_inc(ln_moments[n], 1)
                dve.wait_ge(ln_moments[n], 7 * q + 3)
                nc.vector.tensor_scalar(mo[:, 3], mo[:, 0], 0.5, None, ALU.mult).then_inc(ln_moments[n], 1)
                nc.vector.scalar_tensor_tensor(out=mo[:, 4], in0=mo[:, 1], scalar=0.25, in1=mo[:, 1],
                                               op0=ALU.mult, op1=ALU.mult).then_inc(ln_moments[n], 1)
                nc.vector.tensor_scalar(mo[:, 5], mo[:, 2], 1.0 / D, EPS, ALU.mult, ALU.add)\
                    .then_inc(ln_moments[n], 1)
                dve.wait_ge(ln_moments[n], 7 * q + 6)
                nc.vector.tensor_tensor(var_eps[n][:, :], mo[:, 4], mo[:, 5], ALU.add).then_inc(ln_moments[n], 1)
                dve.wait_ge(ln_rstd[n], q + 1)
                if not first:
                    dve.wait_ge(used, used_value)
                for b in range(QB):
                    nc.vector.tensor_scalar(xn[n][:, b, :], src[:, b, :], moments[n][:, 3, b:b + 1],
                                            rstd[n][:, b:b + 1], ALU.subtract, ALU.mult).then_inc(ln_out[n], 1)

            def step(t, front, back):
                u = t - 1
                if front:
                    dve.wait_ge(x_loaded, 16 * t + 16)
                    layer_norm(0, x_in, t, xnT_made, t)
                    dve.wait_ge(q_hi, t + 1)
                    if back:
                        dve.wait_ge(q_lo, u + 1)
                    nc.vector.tensor_tensor(q_rest[:, :], proj[1][:, :], q_parts[:, 0, :], ALU.subtract)\
                        .then_inc(q_left, 1)
                    dve.wait_ge(k_hi, t + 1)
                    if back:
                        dve.wait_ge(k_lo, u + 1)
                    nc.vector.tensor_tensor(k_rest[:, :], proj[0][:, :], k_parts[:, 0, :], ALU.subtract)\
                        .then_inc(k_left, 1)
                    dve.wait_ge(v_made, t + 1)
                    if back:
                        dve.wait_ge(pv_done, 8 * u + 8)
                    for b in range(QB):
                        dst = v_heads[:, b].rearrange("p (g i) c -> p g (i c)", i=4)
                        nc.vector.tensor_copy(
                            v_diag(v_heads, b, P),
                            proj[1][:, D * b:D * b + D].rearrange("p (g i d) -> p g i d", i=4, d=DH))\
                            .then_inc(v_ready, 1)

                def max_cross(k):
                    b, a = k // 2, k % 2
                    dve.wait_ge(cs_made, 8 * u + k + 1)
                    if k == 0 and (True):
                        dve.wait_ge(cmaxT_made, u)
                    src = score[k % 2][:, :].rearrange("p (n c) -> p n c", n=2)[:, :, 0:4 * TC]\
                        .rearrange("p n (i k) -> p n i k", k=TC)
                    nc.vector.tensor_reduce(cneg_max[:, a, :, b].rearrange("p (n i) -> p n i", n=2), src,
                                            AX_X, ALU.max, negate=True).then_inc(cmax_taken, 1)

                def max_self(k):
                    dve.wait_ge(s_made, 6 * t + k + 1)
                    if k == 0 and back:
                        dve.wait_ge(maxT_made, u + 1)
                    bb, kind = 2 * (k // 3), k % 3
                    if kind < 2:
                        nc.vector.tensor_reduce(neg_max[:, 1, :, bb + kind],
                                                score[k % 2][:, :].rearrange("p (g k) -> p g k", g=G),
                                                AX_X, ALU.max, negate=True).then_inc(max_taken, 1)
                    else:
                        nc.vector.tensor_reduce(neg_max[:, 0, :, bb:bb + 2].rearrange("p g b -> p b g"),
                                                score[k % 2][:, :].rearrange("p (b g k) -> p b g k", b=2, g=G),
                                                AX_X, ALU.max, negate=True).then_inc(max_taken, 1)

                if back:
                    for k in range(8):
                        max_cross(k)
                if front:
                    max_self(0)
                    max_self(1)
                if back:
                    dve.wait_ge(cmax_hi_ready, u + 1)
                    nc.vector.tensor_tensor(cmax_mid[:, :], cmax_f[:, :], cmax_hi[:, :], ALU.subtract)\
                        .then_inc(cmax_mid_ready, 1)
                if front:
                    for k in range(2, 6):
                        max_self(k)
                    dve.wait_ge(max_hi_ready, t + 1)
                    nc.vector.tensor_tensor(max_mid[:, :, :], max_f[:, :, :], max_hi[:, :, :], ALU.subtract)\
                        .then_inc(max_mid_ready, 1)

                def normalize(b, q, pv, inv, inv_ready, att, ready, used, used_value):
                    dve.wait_ge(pv, 8 * q + 2 * b + 2)
                    if b >= 2:
                        dve.wait_ge(ready, 4 * q + b - 1)
                    nc.vector.reciprocal(inv[:, b % 2, :], sums[b % 2][:, 1, :]).then_inc(inv_ready, 1)
                    dve.wait_ge(inv_ready, 4 * q + b + 1)
                    if used is not None and b == 0:
                        dve.wait_ge(used, used_value)
                    nc.vector.tensor_tensor(att[:, b, :], sums[b % 2][:, 0, :], inv[:, b % 2, :], ALU.mult)\
                        .then_inc(ready, 1)

                if back:
                    for b in range(QB):
                        normalize(b, u, cpv_done, cden_inv, cden_ready, cattT, catt_ready,
                                  co_made, u)
                    dve.wait_ge(co_made, u + 1)
                    dve.wait_ge(x1b_ready, u + 1)
                    dve.wait_ge(y_ready, u)
                    dve.wait_ge(ln_out[2], QB * u)
                    nc.vector.tensor_tensor(x2[:, :, :], proj[0][:, :].rearrange("p (b d) -> p b d", b=QB),
                                            x1b[:, :, :], ALU.add).then_inc(x2_ready, 1)
                    dve.wait_ge(x2_ready, u + 1)
                    layer_norm(2, x2, u, xeT_made, u)
                if front:
                    dve.wait_ge(ck_hi, t + 1)
                    if back:
                        dve.wait_ge(ck_lo, u + 1)
                    nc.vector.scalar_tensor_tensor(out=ck_rest[:, :], in0=proj[0][:, 0:NC],
                                                   scalar=bias_cols[:, 1:2], in1=ck_parts[:, 0, :],
                                                   op0=ALU.add, op1=ALU.subtract).then_inc(ck_left, 1)
                    dve.wait_ge(cv_made, t + 1)
                    if back:
                        dve.wait_ge(cpv_done, 8 * u + 8)
                    for b in range(QB):
                        nc.vector.tensor_copy(
                            v_diag(cv_heads, b, TC),
                            proj[1][0:TC, D * b:D * b + D].rearrange("p (g i d) -> p g i d", i=4, d=DH))\
                            .then_inc(cv_ready, 1)
                if back:
                    dve.wait_ge(xeT_ready, u + 1)
                    dve.wait_ge(fr_made, u)
                    dve.wait_ge(mix_ready, 2 * u)
                    for n in (1, 0):
                        nc.vector.tensor_scalar(mix_a[:, n], xeT[:, :, 0:T], mu_rest[:, n:n + 1], None, ALU.mult)\
                            .then_inc(mix_part, 1)
                        dve.wait_ge(mix_part, 2 * u + (2 - n))
                        nc.vector.scalar_tensor_tensor(out=mixed[:, n], in0=xeT[:, :, 1:T + 1],
                                                       scalar=mu[:, n:n + 1], in1=mix_a[:, n],
                                                       op0=ALU.mult, op1=ALU.add).then_inc(mix_ready, 1)
                    dve.wait_ge(gate_e_ready, u + 1)
                    nc.vector.tensor_scalar(gate_d[:, :], gate_e[:, :], 1.0, None, ALU.add).then_inc(gate_d_ready, 1)
                    dve.wait_ge(gate_d_ready, u + 1)
                    nc.vector.reciprocal(gate[:, :], gate_d[:, :]).then_inc(gate_ready, 1)
                    dve.wait_ge(gate_ready, u + 1)
                    dve.wait_ge(fv_made, u + 1)
                    dve.wait_ge(y_ready, u)
                    nc.vector.tensor_tensor(y_gated[:, :], proj[1][:, :], gate[:, :], ALU.mult)\
                        .then_inc(y_gated_ready, 1)
                if front:
                    for b in range(QB):
                        normalize(b, t, pv_done, den_inv, den_ready, attT, att_ready,
                                  o_made if back else None, t)
                    dve.wait_ge(o_made, t + 1)
                    if back:
                        dve.wait_ge(x1b_ready, u + 1)
                        dve.wait_ge(ln_out[1], QB * t)
                    nc.vector.tensor_tensor(x1[:, :, :], proj[0][:, :].rearrange("p (b d) -> p b d", b=QB),
                                            x_in[:, :, :], ALU.add).then_inc(x1_ready, 1)
                    dve.wait_ge(x1_ready, t + 1)
                    layer_norm(1, x1, t, xcT_made, t)
                    dve.wait_ge(cq_hi, t + 1)
                    if back:
                        dve.wait_ge(cq_lo, u + 1)
                    nc.vector.scalar_tensor_tensor(out=cq_rest[:, :], in0=proj[0][:, :],
                                                   scalar=bias_cols[:, 0:1], in1=cq_parts[:, 0, :],
                                                   op0=ALU.add, op1=ALU.subtract).then_inc(cq_left, 1)

            def v_diag(heads, b, rows):
                flat = heads[0:rows, b].rearrange("p (g i) c -> p g (i c)", i=4)
                skew = bass.AP(tensor=flat.tensor, offset=flat.offset,
                               ap=[list(flat.ap[0]), [128, 4], [40, 4], [1, DH]])
                return skew

            schedule(dve, step)

        @block.tensor
        def _(pe):
            pe.wait_ge(ident_made, 1)
            pe.wait_ge(w_in, 176)
            for n in (CQ, CK, CV, CO, FR, FK, FV):
                j = n - CQ
                last = nc.tensor.transpose(proj[j // 4][:, P * (j % 4):P * (j % 4) + P], w_raw[:, n, :], ident[:, :])
                if n in (CO, FV):
                    last.then_inc(w_turned, 1)
            pe.wait_ge(bias_permuted, 3)
            pe.wait_ge(consts_made, 9)
            for n in range(3):
                nc.tensor.matmul(score[0][:, n:n + 1], bias_perm[0:1, n, :], one[0:1, 0:1], start=True, stop=True)\
                    .then_inc(bias_turned, 1)
            pe.wait_ge(bias_wide, 1)
            pe.wait_ge(w_ready, 11)
            nc.tensor.matmul(score[0][:, 0:P], cbv_wide[:, :], wT[:, CO, :], start=True, stop=True)\
                .then_inc(out_bias_mm, 1)
            pe.wait_ge(consts_made, 23)
            pe.wait_ge(setup_dve, 8)

            def turn(dst, src, rows):
                for b in range(QB):
                    last = nc.tensor.transpose(dst[:, rows * b:rows * b + rows], src[0:rows, b, :],
                                               ident[0:rows, 0:rows])
                return last

            def score_max_self(k, t):
                bb, kind = 2 * (k // 3), k % 3
                dst = score[k % 2]
                if kind < 2:
                    b = bb + kind
                    for n in range(2):
                        nc.tensor.matmul(dst[:, 512 * n:512 * n + 512], pick_hi[:, :, :], band[:, :, :],
                                         start=True, stop=False)
                    for g in range(G):
                        for a in range(2):
                            last = nc.tensor.matmul(dst[HALF * a:HALF * a + HALF, T * g:T * g + T],
                                                    q_stack[0:NSTACK, a, g, b, HALF:T],
                                                    k_stack[0:NSTACK, g, b, :], start=False, stop=(g % 4 == 3))
                else:
                    for n in range(2):
                        nc.tensor.matmul(dst[:, 512 * n:512 * n + 512], pick_lo[:, :, :], band_lo[:, :, :],
                                         start=True, stop=False)
                        for g in range(G):
                            c = 512 * n + HALF * g
                            for a in range(2):
                                last = nc.tensor.matmul(dst[HALF * a:HALF * a + HALF, c:c + HALF],
                                                        q_stack[0:NSTACK, a, g, bb + n, 0:HALF],
                                                        k_stack[0:NSTACK, g, bb + n, 0:HALF],
                                                        start=False, stop=(g == G - 1))
                last.then_inc(s_made, 1)

            def attend(k, probs_in, values, ready, ready_value, done):
                b, j = k // 2, k % 2
                pe.wait_ge(ready, ready_value)
                dst = sums[b % 2]
                for a in range(2):
                    for g in range(4):
                        nc.tensor.matmul(dst[32 * g:32 * g + 32, 0, :], values[:, b, 4 * g + 2 * j + a, :],
                                         probs_in[:, k % 2, g, a, :], start=(j == 0 and a == 0),
                                         stop=(j == 1 and a == 1), tile_position=(0, 32 * g),
                                         skip_group_check=True)
                for a in range(2):
                    for g in range(4):
                        last = nc.tensor.matmul(dst[32 * g:32 * g + 32, 1, :], head_ones[:, 2 * j + a, :],
                                                probs_in[:, k % 2, g, a, :], start=False,
                                                stop=(j == 1 and a == 1), tile_position=(0, 32 * g),
                                                skip_group_check=True)
                last.then_inc(done, 1)

            def project_out(att, w, ready, q, dst, made):
                for b in range(QB):
                    pe.wait_ge(ready, QB * q + b + 1)
                    last = nc.tensor.matmul(dst[:, D * b:D * b + D], att[:, b, :], wT[:, w, :],
                                            start=True, stop=True)
                last.then_inc(made, 1)

            def step(t, front, back):
                u = t - 1
                if front:
                    pe.wait_ge(ln_out[0], QB * t + QB)
                    if back:
                        pe.wait_ge(cq_left, u + 1)
                    turn(proj[0], xn[0], T).then_inc(xnT_made, 1)
                    pe.wait_ge(xnT_ready, t + 1)
                    if back:
                        pe.wait_ge(xcT_ready, u + 1)
                    nc.tensor.matmul(proj[1][:, :], wT[:, SQ, :], xnT[:, :], start=True, stop=True)\
                        .then_inc(q_made, 1)
                    nc.tensor.matmul(proj[0][:, :], wT[:, SK, :], xnT[:, :], start=True, stop=True)\
                        .then_inc(k_made, 1)
                    pe.wait_ge(q_left, t + 1)
                    for b in range(QB):
                        last = nc.tensor.matmul(proj[1][:, D * b:D * b + D], xnT[:, T * b:T * b + T], wT[:, SV, :],
                                                start=True, stop=True)
                    last.then_inc(v_made, 1)
                if back:
                    pe.wait_ge(cq_stacked, 96 * u + 96)
                    pe.wait_ge(ck_stacked, 192 * u + 192)
                    pe.wait_ge(cbias_in, 16 * u + 16)
                    for k in range(8):
                        b, a = k // 2, k % 2
                        if k < 2:
                            pe.wait_ge(exp_done, 8 * u + 7 + k)
                        else:
                            pe.wait_ge(cmax_taken, 8 * u + k - 1)
                        for g in range(G):
                            c = 512 * (g // 4) + TC * (g % 4)
                            last = nc.tensor.matmul(score[k % 2][:, c:c + TC], cq_stack[0:SHIFT_CROSS, a, g, b, :],
                                                    ck_stack[0:SHIFT_CROSS, g, b, :], start=True, stop=True)
                        last.then_inc(cs_made, 1)

                def self_slot(k):
                    if k >= 2:
                        pe.wait_ge(max_taken, 6 * t + k - 1)
                    elif back:
                        pe.wait_ge(cmax_taken, 8 * u + 7 + k)
                    score_max_self(k, t)

                if front:
                    pe.wait_ge(q_stacked, 96 * t + 96)
                    pe.wait_ge(k_stacked, 192 * t + 192)
                    self_slot(0)
                    self_slot(1)
                if back:
                    pe.wait_ge(cmax_taken, 8 * u + 8)
                    if front:
                        pe.wait_ge(k_left, t + 1)
                    else:
                        pe.wait_ge(cq_left, u + 1)
                    nc.tensor.transpose(proj[0][:, 0:T], cneg_max[:, :, :, :], ident[:, :])\
                        .then_inc(cmaxT_made, 1)
                if front:
                    for k in range(2, 6):
                        self_slot(k)

                def cross_scores(k):
                    b, j = k // 2, k % 2
                    if k >= 2:
                        pe.wait_ge(cexp_done, 8 * u + k - 1)
                    elif front:
                        pe.wait_ge(max_taken, 6 * t + 5 + k)
                    else:
                        pe.wait_ge(cmax_taken, 8 * u + 7 + k)
                    for i in range(4):
                        g = 2 * i + j
                        last = nc.tensor.matmul(score[k % 2][0:TC, 256 * i:256 * i + 256], ck_stack[:, g, b, :],
                                                cq_stack[:, :, g, b, :], start=True, stop=True)
                    last.then_inc(csT_made, 1)

                def attend_cross(k):
                    b = k // 2
                    if k % 2 == 0:
                        if b < 2:
                            pe.wait_ge(att_ready, 4 * u + 3 + b)
                        else:
                            pe.wait_ge(catt_ready, 4 * u + b - 1)
                    attend(k, cprobs, cv_heads, cexp_done, 8 * u + k + 1, cpv_done)

                if back:
                    pe.wait_ge(cshift_in, 64 * u + 64)
                    cross_scores(0)
                if front:
                    pe.wait_ge(max_taken, 6 * t + 6)
                    pe.wait_ge(v_ready, 4 * t + 4)
                    nc.tensor.transpose(proj[1][:, 0:T], neg_max[:, :, :, :], ident[:, :])\
                        .then_inc(maxT_made, 1)
                if back:
                    pe.wait_ge(cv_ready, 4 * u + 4)
                    cross_scores(1)
                    for k in range(8):
                        attend_cross(k)
                        if k + 2 < 8:
                            cross_scores(k + 2)
                    pe.wait_ge(cmax_f_ready, u + 1)
                    project_out(cattT, CO, catt_ready, u, proj[0], co_made)
                if front:
                    pe.wait_ge(ctx_loaded, 16 * t + 16)
                    pe.wait_ge(max_f_ready, 2 * t + 2)
                    turn(proj[1], ctx_in, TC).then_inc(ctxT_made, 1)
                    pe.wait_ge(ctxT_ready, t + 1)
                    if back:
                        pe.wait_ge(x2_ready, u + 1)
                    nc.tensor.matmul(proj[0][:, 0:NC], wT[:, CK, :], ctxT[:, :], start=True, stop=True)\
                        .then_inc(ck_made, 1)
                    for b in range(QB):
                        last = nc.tensor.matmul(proj[1][0:TC, D * b:D * b + D], ctxT[:, TC * b:TC * b + TC],
                                                wT[:, CV, :], start=True, stop=True)
                    last.then_inc(cv_made, 1)
                if back:
                    pe.wait_ge(ln_out[2], QB * u + QB)
                    if front:
                        pe.wait_ge(ck_left, t + 1)
                    else:
                        pe.wait_ge(x2_ready, u + 1)
                    turn(proj[0], xn[2], T).then_inc(xeT_made, 1)
                    pe.wait_ge(mix_ready, 2 * u + 1)
                    if front:
                        pe.wait_ge(cv_ready, 4 * t + 4)
                    nc.tensor.matmul(proj[1][:, :], wT[:, FK, :], mixed[:, 1].rearrange("p b t -> p (b t)"),
                                     start=True, stop=True).then_inc(fk_made, 1)
                    pe.wait_ge(mix_ready, 2 * u + 2)
                    pe.wait_ge(xeT_ready, u + 1)
                    for b in range(QB):
                        last = nc.tensor.matmul(proj[0][:, D * b:D * b + D], mixed[:, 0, b, :], wT[:, FR, :],
                                                start=True, stop=True)
                    last.then_inc(fr_made, 1)
                    pe.wait_ge(k_act_ready, u + 1)
                    pe.wait_ge(relu_ready, u + 1)
                    for b in range(QB):
                        last = nc.tensor.matmul(proj[1][:, D * b:D * b + D], k_act[:, b, :], wT[:, FV, :],
                                                start=True, stop=True)
                    last.then_inc(fv_made, 1)

                def self_scores(k):
                    b, j = k // 2, k % 2
                    if k >= 2:
                        pe.wait_ge(exp_done, 8 * t + k - 1)
                    elif back:
                        pe.wait_ge(cexp_done, 8 * u + 7 + k)
                    else:
                        pe.wait_ge(max_taken, 6 * t + 5 + k)
                    for n in range(2):
                        nc.tensor.matmul(score[k % 2][:, 512 * n:512 * n + 512], band[:, 0, :], ident_bf[:, :, :],
                                         start=True, stop=False)
                    for i in range(4):
                        g = 2 * i + j
                        last = nc.tensor.matmul(score[k % 2][:, 256 * i:256 * i + 256], k_stack[:, g, b, :],
                                                q_stack[:, :, g, b, :], start=False, stop=(i % 2 == 1))
                    last.then_inc(sT_made, 1)

                def attend_self(k):
                    b = k // 2
                    if k % 2 == 0:
                        if b >= 2:
                            pe.wait_ge(att_ready, 4 * t + b - 1)
                        elif back:
                            pe.wait_ge(catt_ready, 4 * u + 3 + b)
                    attend(k, probs, v_heads, exp_done, 8 * t + k + 1, pv_done)

                if front:
                    pe.wait_ge(shift_in, 64 * t + 64)
                    self_scores(0)
                    self_scores(1)
                    for k in range(8):
                        attend_self(k)
                        if k + 2 < 8:
                            self_scores(k + 2)
                    if back:
                        pe.wait_ge(gate_e_ready, u + 1)
                    else:
                        pe.wait_ge(ck_left, t + 1)
                    project_out(attT, SO, att_ready, t, proj[0], o_made)
                    pe.wait_ge(ln_out[1], QB * t + QB)
                    if back:
                        pe.wait_ge(y_gated_ready, u + 1)
                    else:
                        pe.wait_ge(cv_ready, 4 * t + 4)
                    turn(proj[1], xn[1], T).then_inc(xcT_made, 1)
                    pe.wait_ge(xcT_ready, t + 1)
                    pe.wait_ge(x1_ready, t + 1)
                    nc.tensor.matmul(proj[0][:, :], wT[:, CQ, :], xcT[:, :], start=True, stop=True)\
                        .then_inc(cq_made, 1)

            schedule(pe, step)


_INS = ['x', 'ctx_1024', 'mask_BxS2_ik1', 'L0_attn_Wq', 'L0_attn_Wk', 'L0_attn_Wv', 'L0_attn_Wo',
        'L0_xattn_Wq', 'L0_xattn_bq', 'L0_xattn_Wk', 'L0_xattn_bk', 'L0_xattn_Wv', 'L0_xattn_bv',
        'L0_xattn_Wo', 'L0_xattn_bo', 'L0_ffn_W_r', 'L0_ffn_W_k', 'L0_ffn_W_v', 'L0_ffn_mu_r', 'L0_ffn_mu_k']
_OUTS = [((BATCH, T, D), 'float32')]


def kernel(**inputs):
    import numpy as _np
    import concourse.bacc as _bacc
    from concourse import mybir as _mybir
    from concourse.bass_utils import run_bass_kernel_spmd as _run

    nc = _bacc.Bacc("TRN2", target_bir_lowering=False, num_devices=1)
    arrays, args = {}, []
    for name in _INS:
        a = _np.ascontiguousarray(inputs[name])
        arrays[f"in_{name}_dram"] = a
        args.append(nc.dram_tensor(f"in_{name}_dram", a.shape, _mybir.dt.from_np(a.dtype), kind="ExternalInput").ap())
    for i, (shape, dtype) in enumerate(_OUTS):
        dt = _mybir.dt.from_np(_np.dtype(dtype))
        args.append(nc.dram_tensor(f"out_{i}_dram", shape, dt, kind="ExternalOutput").ap())
    decoder_layer(nc, *args)
    r = _run(nc, [arrays], core_ids=[0])
    got = tuple(r.results[0][f"out_{i}_dram"] for i in range(len(_OUTS)))
    return got[0]
```

```python
from contextlib import ExitStack

import concourse.bass as bass
from concourse import mybir

F32 = mybir.dt.float32
BF16 = mybir.dt.bfloat16
I32 = mybir.dt.int32
ALU = mybir.AluOpType
ACT = mybir.ActivationFunctionType
AX_X = mybir.AxisListType.X

P = 128
BATCH, T, D = 64, 128, 128
TC = 77
H, DH = 16, 8
G = H // 2
QB = 4
NQ = BATCH // QB
NT, NC = QB * T, QB * TC
WIN = 64
HALF = T // 2
SCALE = float(DH) ** -0.5
EPS = 1e-5
MASKED = -1e30
MASK_WEIGHT = -100.0

QPART = (0, 1, 2, 0, 1, 0)
KPART = (0, 0, 0, 1, 1, 2)
NSTACK = 2 * len(QPART) * DH
SHIFT_SELF = NSTACK
BIAS_CROSS = NSTACK
SHIFT_CROSS = NSTACK + 3


def decoder_layer(nc, x, ctx, mask, wq, wk, wv, wo, cwq, cbq, cwk, cbk, cwv, cbv, cwo, cbo,
                  fwr, fwk, fwv, mu_r, mu_k, out):
    x_quads = x.rearrange("(n b) t d -> n t b d", b=QB)
    out_quads = out.rearrange("(n b) t d -> n t b d", b=QB)
    ctx_quads = ctx.rearrange("(n b) s d -> n s b d", b=QB)

    def scratch(name, shape):
        return nc.dram_tensor(name, shape, BF16).ap()

    q_scr = scratch("q_scr", [2, 3, DH, G, NT])
    k_scr = scratch("k_scr", [2, 3, DH, G, NT])
    cq_scr = scratch("cq_scr", [2, 3, DH, G, NT])
    ck_scr = scratch("ck_scr", [2, 3, DH, G, NC])
    bias_scr = scratch("bias_scr", [3, NQ, G, NC])
    bias_quads = bias_scr.rearrange("c n g s -> n c (g s)")

    with ExitStack() as stack:
        def sb(name, shape, dt=F32):
            return stack.enter_context(nc.sbuf_tensor(name, shape, dt))

        def sem(name):
            return stack.enter_context(nc.semaphore(name))

        ident = sb("ident", [P, P])
        ident_bf = sb("ident_bf", [P, 4, P], BF16)
        band = sb("band", [P, 4, P], BF16)
        band_lo = sb("band_lo", [P, G, HALF], BF16)
        pick_hi = sb("pick_hi", [P, 2, HALF], BF16)
        pick_lo = sb("pick_lo", [P, 2, HALF], BF16)
        head_ones = sb("head_ones", [P, 4, 32])
        one = sb("one", [P, P])
        neg_half = sb("neg_half", [P, QB])
        w_raw = sb("w_raw", [P, 11, P])
        wT = sb("wT", [P, 11, P])
        (SQ, SK, SV, SO, CQ, CK, CV, CO, FR, FK, FV) = range(11)
        bias_rows = sb("bias_rows", [1, 3, P])
        bias_perm = sb("bias_perm", [1, 3, P])
        bias_cols = sb("bias_cols", [P, 3])
        cbv_wide = sb("cbv_wide", [P, P])
        cbo_wide = sb("cbo_wide", [P, P])
        out_bias = sb("out_bias", [P, P])
        mu = sb("mu", [P, 2])
        mu_rest = sb("mu_rest", [P, 2])
        mask_in = sb("mask_in", [NQ, NC], I32)
        mask_f = sb("mask_f", [NQ, NC])
        mask_r = sb("mask_r", [NQ, NC])
        mask_parts = sb("mask_parts", [NQ, 3, NC], BF16)

        x_in = sb("x_in", [P, QB, D])
        x_res = sb("x_res", [P, QB, D])
        stats = [sb(f"stats{n}", [P, QB, 6]) for n in range(3)]
        moments = [sb(f"moments{n}", [P, 6, QB]) for n in range(3)]
        var_eps = [sb(f"var_eps{n}", [P, QB]) for n in range(3)]
        rstd = [sb(f"rstd{n}", [P, QB]) for n in range(3)]
        xn = [sb(f"xn{n}", [P, QB, D]) for n in range(3)]
        xnT = sb("xnT", [P, NT])
        q_parts = sb("q_parts", [P, 3, NT], BF16)
        k_parts = sb("k_parts", [P, 3, NT], BF16)
        q_rest = sb("q_rest", [P, NT])
        k_rest = sb("k_rest", [P, NT])
        q_stack = sb("q_stack", [P, 2, G, QB, T], BF16)
        k_stack = sb("k_stack", [P, G, QB, T], BF16)
        v_heads = sb("v_heads", [P, QB, H, 32])
        neg_max = sb("neg_max", [P, 4, G, QB])
        max_f = sb("max_f", [G * QB, 2, T])
        max_hi = sb("max_hi", [G * QB, 2, T], BF16)
        max_mid = sb("max_mid", [G * QB, 2, T], BF16)
        probs = sb("probs", [P, 2, 4, 2, T])
        den_inv = sb("den_inv", [P, 2, T])
        attT = sb("attT", [P, QB, T])
        x1 = sb("x1", [P, QB, D])
        x1b = sb("x1b", [P, QB, D])

        ctx_in = sb("ctx_in", [TC, QB, D])
        ctxT = sb("ctxT", [P, NC])
        xcT = sb("xcT", [P, NT])
        cq_parts = sb("cq_parts", [P, 3, NT], BF16)
        ck_parts = sb("ck_parts", [P, 3, NC], BF16)
        cq_rest = sb("cq_rest", [P, NT])
        ck_rest = sb("ck_rest", [P, NC])
        cq_stack = sb("cq_stack", [P, 2, G, QB, T], BF16)
        ck_stack = sb("ck_stack", [P, G, QB, TC], BF16)
        cv_heads = sb("cv_heads", [P, QB, H, 32])
        cneg_max = sb("cneg_max", [P, 4, G, QB])
        cmax_f = sb("cmax_f", [2 * G * QB, T])
        cmax_hi = sb("cmax_hi", [2 * G * QB, T], BF16)
        cmax_mid = sb("cmax_mid", [2 * G * QB, T], BF16)
        cprobs = sb("cprobs", [P, 2, 4, 2, T])
        cden_inv = sb("cden_inv", [P, 2, T])
        cattT = sb("cattT", [P, QB, T])
        x2 = sb("x2", [P, QB, D])
        xeT = sb("xeT", [P, QB, T + 1])
        mix_a = sb("mix_a", [P, 2, QB, T])
        mixed = sb("mixed", [P, 2, QB, T])
        k_relu = sb("k_relu", [P, NT])
        k_act = sb("k_act", [P, QB, T])
        gate_tanh = sb("gate_tanh", [P, NT])
        y_gated = sb("y_gated", [P, NT])
        y_out = sb("y_out", [P, QB, D])

        score = [stack.enter_context(nc.psum_tensor(f"score{n}", [P, 1024], F32)) for n in range(2)]
        sums = [stack.enter_context(nc.psum_tensor(f"sums{n}", [P, 4, T], F32)) for n in range(2)]
        proj = [stack.enter_context(nc.psum_tensor(f"proj{n}", [P, 512], F32)) for n in range(2)]

        w_in = sem("w_in")
        small_in = sem("small_in")
        mask_loaded = sem("mask_loaded")
        ident_zero = sem("ident_zero")
        ident_made = sem("ident_made")
        consts_made = sem("consts_made")
        zeros_made = sem("zeros_made")
        ones_rows = sem("ones_rows")
        w_turned = sem("w_turned")
        w_ready = sem("w_ready")
        bias_permuted = sem("bias_permuted")
        bias_turned = sem("bias_turned")
        bias_ready = sem("bias_ready")
        bias_wide = sem("bias_wide")
        out_bias_mm = sem("out_bias_mm")
        setup_dve = sem("setup_dve")
        bias_stored = sem("bias_stored")

        x_loaded = sem("x_loaded")
        x_kept = sem("x_kept")
        ln_stats = [sem(f"ln_stats{n}") for n in range(3)]
        ln_moments = [sem(f"ln_moments{n}") for n in range(3)]
        ln_rstd = [sem(f"ln_rstd{n}") for n in range(3)]
        ln_out = [sem(f"ln_out{n}") for n in range(3)]
        xnT_made = sem("xnT_made")
        xnT_ready = sem("xnT_ready")
        q_made = sem("q_made")
        q_hi = sem("q_hi")
        q_left = sem("q_left")
        q_mid = sem("q_mid")
        q_lo = sem("q_lo")
        k_made = sem("k_made")
        k_hi = sem("k_hi")
        k_left = sem("k_left")
        k_mid = sem("k_mid")
        k_lo = sem("k_lo")
        v_made = sem("v_made")
        v_ready = sem("v_ready")
        q_stored = sem("q_stored")
        k_stored = sem("k_stored")
        q_stacked = sem("q_stacked")
        k_stacked = sem("k_stacked")
        s_made = sem("s_made")
        max_taken = sem("max_taken")
        maxT_made = sem("maxT_made")
        max_f_ready = sem("max_f_ready")
        max_hi_ready = sem("max_hi_ready")
        max_mid_ready = sem("max_mid_ready")
        shift_in = sem("shift_in")
        sT_made = sem("sT_made")
        exp_done = sem("exp_done")
        pv_done = sem("pv_done")
        den_ready = sem("den_ready")
        att_ready = sem("att_ready")
        o_made = sem("o_made")
        x1_ready = sem("x1_ready")
        x1b_ready = sem("x1b_ready")

        ctx_loaded = sem("ctx_loaded")
        ctxT_made = sem("ctxT_made")
        ctxT_ready = sem("ctxT_ready")
        cbias_in = sem("cbias_in")
        xcT_made = sem("xcT_made")
        xcT_ready = sem("xcT_ready")
        cq_made = sem("cq_made")
        cq_hi = sem("cq_hi")
        cq_left = sem("cq_left")
        cq_mid = sem("cq_mid")
        cq_lo = sem("cq_lo")
        ck_made = sem("ck_made")
        ck_hi = sem("ck_hi")
        ck_left = sem("ck_left")
        ck_mid = sem("ck_mid")
        ck_lo = sem("ck_lo")
        cv_made = sem("cv_made")
        cv_ready = sem("cv_ready")
        cq_stored = sem("cq_stored")
        ck_stored = sem("ck_stored")
        cq_stacked = sem("cq_stacked")
        ck_stacked = sem("ck_stacked")
        cs_made = sem("cs_made")
        cmax_taken = sem("cmax_taken")
        cmaxT_made = sem("cmaxT_made")
        cmax_f_ready = sem("cmax_f_ready")
        cmax_hi_ready = sem("cmax_hi_ready")
        cmax_mid_ready = sem("cmax_mid_ready")
        cshift_in = sem("cshift_in")
        csT_made = sem("csT_made")
        cexp_done = sem("cexp_done")
        cpv_done = sem("cpv_done")
        cden_ready = sem("cden_ready")
        catt_ready = sem("catt_ready")
        co_made = sem("co_made")
        x2_ready = sem("x2_ready")
        xeT_made = sem("xeT_made")
        xeT_ready = sem("xeT_ready")
        mix_part = sem("mix_part")
        mix_ready = sem("mix_ready")
        fk_made = sem("fk_made")
        relu_ready = sem("relu_ready")
        k_act_ready = sem("k_act_ready")
        fr_made = sem("fr_made")
        gate_tanh_ready = sem("gate_tanh_ready")
        fv_made = sem("fv_made")
        y_gated_ready = sem("y_gated_ready")
        y_ready = sem("y_ready")
        y_stored = sem("y_stored")

        block = stack.enter_context(nc.Block())

        def schedule(eng, step):
            step(-1, False, False, True)
            step(0, True, False, True)
            step(1, True, True, True)
            with eng.Fori(2, NQ - 1) as s:
                step(s, True, True, True)
            step(NQ - 1, True, True, False)
            step(NQ, False, True, False)

        def later(q):
            return not isinstance(q, int) or q > 0

        @block.sync
        def _(sp):
            for n, w in enumerate((wq, wk, wv, wo, cwq, cwk, cwv, cwo, fwr, fwk, fwv)):
                sp.dma_start(w_raw[:, n, :], w).then_inc(w_in, 16)
            for n, b in enumerate((cbq, cbk, cbv)):
                sp.dma_start(bias_rows[:, n, :], b.rearrange("(o d) -> o d", o=1)).then_inc(small_in, 16)
            for n, m in enumerate((mu_r, mu_k)):
                sp.dma_start(mu[:, n:n + 1], m.rearrange("(d o) -> d o", o=1)).then_inc(small_in, 16)
            sp.dma_start(cbo_wide[:, :], cbo.partition_broadcast(P)).then_inc(small_in, 16)
            sp.dma_start(mask_in[:, :], mask.rearrange("(n b) s -> n (b s)", b=QB)).then_inc(mask_loaded, 16)
            sp.wait_ge(zeros_made, 4)
            for r in range(4):
                sp.dma_start(cq_stack[BIAS_CROSS:BIAS_CROSS + 3, r // 2, 4 * (r % 2):4 * (r % 2) + 4]
                             .rearrange("p g b q -> p (g b q)"),
                             ck_stack[BIAS_CROSS:BIAS_CROSS + 3]
                             .rearrange("p g b k -> p (g b k)")[:, 0:2048]).then_inc(ones_rows, 16)
            sp.wait_ge(setup_dve, 10)
            for g in range(G):
                sp.dma_start(bias_scr[:, :, g, :].rearrange("c n s -> n c s"), mask_parts[:, :, :])\
                    .then_inc(bias_stored, 16)

            def store_parts(parts, scr, stored):
                for a in range(2):
                    sp.dma_start(scr[a].rearrange("p d g t -> (d g) p t"),
                                 parts[HALF * a:HALF * a + HALF]).then_inc(stored, 16)

            def stack_queries(scr, dst, stacked):
                rows = dst.rearrange("p a g b q -> p a (g b q)")
                for a in range(2):
                    for c, n in ((0, 3), (3, 2), (5, 1)):
                        r = 48 * a + DH * c
                        sp.dma_start(rows[r:r + DH * n, a, :],
                                     scr[a, 0:n].rearrange("p d g t -> (p d) (g t)")).then_inc(stacked, 16)

            def stack_keys(scr, dst, stacked):
                rows = dst.rearrange("p g b k -> p (g b k)")
                for a in range(2):
                    for c, part in enumerate(KPART):
                        r = 48 * a + DH * c
                        sp.dma_start(rows[r:r + DH, :],
                                     scr[a, part].rearrange("d g t -> d (g t)")).then_inc(stacked, 16)

            def step(s, body, back, head):
                u, n = s - 1, s + 1
                if head:
                    if body:
                        sp.wait_ge(ln_out[0], QB * n)
                        sp.wait_ge(x_kept, n)
                    sp.dma_start(x_in[:, :, :], x_quads[n] if isinstance(s, int) else x_quads[1:][s]).then_inc(x_loaded, 16)
                if body:
                    sp.wait_ge(max_mid_ready, s + 1)
                    sp.wait_ge(max_hi_ready, s + 1)
                    for a in range(2):
                        for part, src in enumerate((max_hi, max_mid)):
                            r = SHIFT_SELF + 2 * a + part
                            sp.dma_start(q_stack[r:r + 1, a].rearrange("o g b q -> o (g b) q"),
                                         src[:, a, :]).then_inc(shift_in, 16)
                if back:
                    sp.wait_ge(cmax_mid_ready, u + 1)
                    sp.wait_ge(cmax_hi_ready, u + 1)
                    for a in range(2):
                        for part, src in enumerate((cmax_hi, cmax_mid)):
                            r = SHIFT_CROSS + 2 * a + part
                            sp.dma_start(cq_stack[r:r + 1, a].rearrange("o g b q -> o (g b) q"),
                                         src[32 * a:32 * a + 32, :]).then_inc(cshift_in, 16)
                if body:
                    if later(s):
                        sp.wait_ge(ctxT_made, s)
                    sp.dma_start(ctx_in[:, :, :], ctx_quads[s]).then_inc(ctx_loaded, 16)
                if head:
                    sp.wait_ge(q_lo, n + 1)
                    store_parts(q_parts[:, :, :], q_scr, q_stored)
                    sp.wait_ge(k_lo, n + 1)
                    store_parts(k_parts[:, :, :], k_scr, k_stored)
                    if body:
                        sp.wait_ge(sT_made, 8 * s + 8)
                    else:
                        sp.wait_ge(zeros_made, 4)
                    sp.wait_ge(q_stored, 32 * n + 32)
                    stack_queries(q_scr, q_stack[:, :, :, :, :], q_stacked)
                    sp.wait_ge(k_stored, 32 * n + 32)
                    stack_keys(k_scr, k_stack[:, :, :, :], k_stacked)
                if body:
                    sp.wait_ge(cq_lo, s + 1)
                    store_parts(cq_parts[:, :, :], cq_scr, cq_stored)
                    if back:
                        sp.wait_ge(csT_made, 8 * u + 8)
                    else:
                        sp.wait_ge(ones_rows, 64)
                        sp.wait_ge(bias_stored, 16 * G)
                    sp.wait_ge(cq_stored, 32 * s + 32)
                    stack_queries(cq_scr, cq_stack[:, :, :, :, :], cq_stacked)
                    sp.wait_ge(ck_lo, s + 1)
                    store_parts(ck_parts[:, :, :], ck_scr, ck_stored)
                    sp.dma_start(ck_stack[BIAS_CROSS:BIAS_CROSS + 3].rearrange("p g b k -> p (g b k)"),
                                 bias_quads[s]).then_inc(cbias_in, 16)
                    sp.wait_ge(ck_stored, 32 * s + 32)
                    stack_keys(ck_scr, ck_stack[:, :, :, :], ck_stacked)
                if back:
                    sp.wait_ge(y_ready, u + 1)
                    sp.dma_start(out_quads[u], y_out[:, :, :]).then_inc(y_stored, 16)

            schedule(sp, step)
            sp.wait_ge(y_stored, 16 * NQ)

        @block.gpsimd
        def _(pool):
            nc.gpsimd.memset(ident[:, :], 0.0).then_inc(ident_zero, 1)
            nc.gpsimd.memset(band[:, :, :], 0.0).then_inc(ident_zero, 1)
            pool.wait_ge(ident_zero, 2)
            nc.gpsimd.affine_select(out=ident[:, :], in_=ident[:, :], compare_op=ALU.not_equal, fill=1.0,
                                    base=0, pattern=[[-1, P]], channel_multiplier=1).then_inc(ident_made, 1)
            nc.gpsimd.affine_select(out=band[:, :, :], in_=band[:, :, :], compare_op=ALU.is_ge, fill=MASKED,
                                    base=0, pattern=[[0, 4], [-1, P]], channel_multiplier=1)\
                .then_inc(ident_made, 1)
            pool.wait_ge(ident_made, 2)
            nc.gpsimd.affine_select(out=band[:, :, :], in_=band[:, :, :], compare_op=ALU.is_ge, fill=MASKED,
                                    base=WIN - 1, pattern=[[0, 4], [1, P]], channel_multiplier=-1)\
                .then_inc(ident_made, 1)

            def rstd_of(n, q):
                pool.wait_ge(ln_moments[n], 7 * q + 7)
                pool.wait_ge(ln_out[n], QB * q)
                nc.gpsimd.tensor_tensor(rstd[n][:, :], var_eps[n][:, :], neg_half[:, :], ALU.pow)\
                    .then_inc(ln_rstd[n], 1)

            def low_part(parts, rest, left, mid, lo, stored, q):
                if later(q):
                    pool.wait_ge(stored, 32 * q)
                pool.wait_ge(left, q + 1)
                pool.wait_ge(mid, q + 1)
                nc.gpsimd.tensor_tensor(parts[:, 2, :], rest[:, :], parts[:, 1, :], ALU.subtract)\
                    .then_inc(lo, 1)

            def step(s, body, back, head):
                u, n = s - 1, s + 1
                if head:
                    rstd_of(0, n)
                if body:
                    rstd_of(1, s)
                if head:
                    low_part(q_parts, q_rest, q_left, q_mid, q_lo, q_stored, n)
                    low_part(k_parts, k_rest, k_left, k_mid, k_lo, k_stored, n)
                if back:
                    rstd_of(2, u)
                if body:
                    pool.wait_ge(x1_ready, s + 1)
                    if back:
                        pool.wait_ge(x2_ready, u + 1)
                    nc.gpsimd.tensor_tensor(x1b[:, :, :], x1[:, :, :],
                                            out_bias[:, :].unsqueeze(1).to_broadcast([P, QB, D]), ALU.add)\
                        .then_inc(x1b_ready, 1)
                    low_part(cq_parts, cq_rest, cq_left, cq_mid, cq_lo, cq_stored, s)
                    low_part(ck_parts, ck_rest, ck_left, ck_mid, ck_lo, ck_stored, s)
                if back:
                    pool.wait_ge(relu_ready, u + 1)
                    if later(u):
                        pool.wait_ge(fv_made, u)
                    nc.gpsimd.tensor_tensor(k_act[:, :, :], k_relu[:, :].rearrange("p (b t) -> p b t", b=QB),
                                            k_relu[:, :].rearrange("p (b t) -> p b t", b=QB), ALU.mult)\
                        .then_inc(k_act_ready, 1)
                    pool.wait_ge(y_gated_ready, u + 1)
                    if later(u):
                        pool.wait_ge(y_stored, 16 * u)
                    nc.gpsimd.tensor_tensor(y_out[:, :, :], y_gated[:, :].rearrange("p (b d) -> p b d", b=QB),
                                            x2[:, :, :], ALU.add).then_inc(y_ready, 1)

            pool.wait_ge(setup_dve, 8)
            schedule(pool, step)

        @block.scalar
        def _(act):
            act.wait_ge(w_turned, 2)
            for n in (CQ, CK, CV, CO, FR, FK, FV):
                src = proj[(n - CQ) // 4][:, P * ((n - CQ) % 4):P * ((n - CQ) % 4) + P]
                if n in (CQ, CK):
                    nc.scalar.activation(wT[:, n, :].rearrange("p (a d g) -> p a d g", a=2, d=DH),
                                         src.rearrange("p (g a d) -> p a d g", a=2, d=DH), ACT.Copy,
                                         scale=SCALE if n == CQ else 1.0).then_inc(w_ready, 1)
                else:
                    nc.scalar.activation(wT[:, n, :], src, ACT.Copy, scale=0.5 if n == FV else 1.0)\
                        .then_inc(w_ready, 1)

            def high_part(parts, src, made, stored, hi, q, bias=None):
                act.wait_ge(made, q + 1)
                if later(q):
                    act.wait_ge(stored, 32 * q)
                if bias is None:
                    nc.scalar.activation(parts[:, 0, :], src, ACT.Copy).then_inc(hi, 1)
                else:
                    nc.scalar.activation(parts[:, 0, :], src, ACT.Identity, bias=bias).then_inc(hi, 1)

            def mid_part(parts, rest, left, mid, q):
                act.wait_ge(left, q + 1)
                nc.scalar.activation(parts[:, 1, :], rest[:, :], ACT.Copy).then_inc(mid, 1)

            def step(s, body, back, head):
                u, n = s - 1, s + 1
                if body:
                    act.wait_ge(maxT_made, s + 1)
                    if later(s):
                        act.wait_ge(max_mid_ready, s)
                        act.wait_ge(shift_in, 64 * s)
                    for i in range(2):
                        nc.scalar.activation(max_f[:, :, HALF * i:HALF * i + HALF],
                                             proj[0][32 * i:32 * i + 32, 0:T]
                                             .rearrange("p (a q) -> p a q", a=2), ACT.Copy)\
                            .then_inc(max_f_ready, 1)
                    act.wait_ge(max_f_ready, 2 * s + 2)
                    nc.scalar.activation(max_hi[:, :, :], max_f[:, :, :], ACT.Copy).then_inc(max_hi_ready, 1)

                def exp_self(k):
                    act.wait_ge(sT_made, 8 * s + k + 1)
                    if k >= 2:
                        act.wait_ge(pv_done, 8 * s + k - 1)
                    elif later(s):
                        act.wait_ge(pv_done, 8 * s)
                    nc.scalar.activation(probs[:, k % 2].rearrange("p g a q -> p (g a q)"),
                                         score[k % 2][:, :], ACT.Exp).then_inc(exp_done, 1)

                def exp_cross(k):
                    act.wait_ge(csT_made, 8 * u + k + 1)
                    if k >= 2:
                        act.wait_ge(cpv_done, 8 * u + k - 1)
                    elif later(u):
                        act.wait_ge(cpv_done, 8 * u)
                    nc.scalar.activation(cprobs[0:TC, k % 2].rearrange("p g a q -> p (g a q)"),
                                         score[k % 2][0:TC, :], ACT.Exp).then_inc(cexp_done, 1)

                if body:
                    exp_self(0)
                    exp_self(1)
                if back:
                    act.wait_ge(cmaxT_made, u + 1)
                    if later(u):
                        act.wait_ge(cmax_mid_ready, u)
                        act.wait_ge(cshift_in, 64 * u)
                    nc.scalar.activation(cmax_f[:, :], proj[1][0:2 * G * QB, 0:T], ACT.Copy)\
                        .then_inc(cmax_f_ready, 1)
                    act.wait_ge(cmax_f_ready, u + 1)
                    nc.scalar.activation(cmax_hi[:, :], cmax_f[:, :], ACT.Copy).then_inc(cmax_hi_ready, 1)
                if body:
                    for k in range(2, 8):
                        exp_self(k)
                if head:
                    act.wait_ge(xnT_made, n + 1)
                    if later(n):
                        act.wait_ge(v_made, n)
                    nc.scalar.activation(xnT[:, :], proj[1][:, :], ACT.Copy).then_inc(xnT_ready, 1)
                    act.wait_ge(x_loaded, 16 * n + 16)
                    if body:
                        act.wait_ge(x1_ready, s + 1)
                    nc.scalar.activation(x_res[:, :, :], x_in[:, :, :], ACT.Copy).then_inc(x_kept, 1)
                    high_part(q_parts, proj[0][:, :], q_made, q_stored, q_hi, n)
                    high_part(k_parts, proj[1][:, :], k_made, k_stored, k_hi, n)
                    mid_part(q_parts, q_rest, q_left, q_mid, n)
                    mid_part(k_parts, k_rest, k_left, k_mid, n)
                if back:
                    for k in range(8):
                        exp_cross(k)
                if body:
                    act.wait_ge(xcT_made, s + 1)
                    if later(s):
                        act.wait_ge(cq_made, s)
                    nc.scalar.activation(xcT[:, :], proj[0][:, :], ACT.Copy).then_inc(xcT_ready, 1)
                    high_part(cq_parts, proj[1][:, :], cq_made, cq_stored, cq_hi, s, bias_cols[:, 0:1])
                    act.wait_ge(ctxT_made, s + 1)
                    if later(s):
                        act.wait_ge(cv_made, s)
                    nc.scalar.activation(ctxT[:, :], proj[0][:, 0:NC], ACT.Copy).then_inc(ctxT_ready, 1)
                    mid_part(cq_parts, cq_rest, cq_left, cq_mid, s)
                    high_part(ck_parts, proj[1][:, 0:NC], ck_made, ck_stored, ck_hi, s, bias_cols[:, 1:2])
                    mid_part(ck_parts, ck_rest, ck_left, ck_mid, s)
                if back:
                    act.wait_ge(xeT_made, u + 1)
                    act.wait_ge(consts_made, 9)
                    if later(u):
                        act.wait_ge(mix_ready, 2 * u)
                    nc.scalar.activation(xeT[:, :, 1:T + 1], proj[1][:, :].rearrange("p (b t) -> p b t", b=QB),
                                         ACT.Copy).then_inc(xeT_ready, 1)
                    act.wait_ge(fk_made, u + 1)
                    if later(u):
                        act.wait_ge(k_act_ready, u)
                    nc.scalar.activation(k_relu[:, :], proj[0][:, :], ACT.Relu).then_inc(relu_ready, 1)
                    act.wait_ge(fr_made, u + 1)
                    if later(u):
                        act.wait_ge(y_gated_ready, u)
                    nc.scalar.activation(gate_tanh[:, :], proj[1][:, :], ACT.Tanh, scale=0.5)\
                        .then_inc(gate_tanh_ready, 1)

            act.wait_ge(bias_ready, 3)
            schedule(act, step)

        @block.vector
        def _(dve):
            nc.vector.memset(q_stack[:, :, :, :, :], 0.0).then_inc(zeros_made, 1)
            nc.vector.memset(cq_stack[:, :, :, :, :], 0.0).then_inc(zeros_made, 1)
            nc.vector.memset(k_stack[:, :, :, :], 1.0).then_inc(zeros_made, 1)
            nc.vector.memset(ck_stack[:, :, :, :], 1.0).then_inc(zeros_made, 1)
            nc.vector.memset(v_heads[:, :, :, :], 0.0).then_inc(consts_made, 1)
            nc.vector.memset(cv_heads[:, :, :, :], 0.0).then_inc(consts_made, 1)
            nc.vector.memset(cprobs[:, :, :, :, :], 0.0).then_inc(consts_made, 1)
            nc.vector.memset(xeT[:, :, :], 0.0).then_inc(consts_made, 1)
            nc.vector.memset(head_ones[:, :, :], 0.0).then_inc(consts_made, 1)
            nc.vector.memset(one[:, :], 1.0).then_inc(consts_made, 1)
            nc.vector.memset(neg_half[:, :], -0.5).then_inc(consts_made, 1)
            nc.vector.memset(neg_max[:, :, :, :], 0.0).then_inc(consts_made, 1)
            nc.vector.memset(cneg_max[:, :, :, :], 0.0).then_inc(consts_made, 1)
            dve.wait_ge(consts_made, 9)
            for i in range(4):
                nc.vector.memset(head_ones[:, i, DH * i:DH * i + DH], 1.0).then_inc(consts_made, 1)
            dve.wait_ge(ident_made, 3)
            for i in range(4):
                nc.vector.tensor_copy(ident_bf[:, i, :], ident[:, :]).then_inc(consts_made, 1)
            for s in range(2):
                nc.vector.tensor_copy(pick_lo[:, s, :], ident[:, 0:HALF]).then_inc(consts_made, 1)
                nc.vector.tensor_copy(pick_hi[:, s, :], ident[:, HALF:P]).then_inc(consts_made, 1)
            for s in range(2):
                nc.vector.tensor_copy(band_lo[:, 4 * s:4 * s + 4, :], band[:, :, 0:HALF]).then_inc(consts_made, 1)
            dve.wait_ge(w_in, 176)
            nc.vector.tensor_scalar(wT[:, SQ, :].rearrange("p (a d g) -> p a d g", a=2, d=DH),
                                    w_raw[:, SQ, :].rearrange("p (g a d) -> p a d g", a=2, d=DH),
                                    SCALE, None, ALU.mult).then_inc(w_ready, 1)
            nc.vector.tensor_copy(wT[:, SK, :].rearrange("p (a d g) -> p a d g", a=2, d=DH),
                                  w_raw[:, SK, :].rearrange("p (g a d) -> p a d g", a=2, d=DH)).then_inc(w_ready, 1)
            nc.vector.tensor_copy(wT[:, SV, :], w_raw[:, SV, :]).then_inc(w_ready, 1)
            nc.vector.tensor_copy(wT[:, SO, :], w_raw[:, SO, :]).then_inc(w_ready, 1)
            dve.wait_ge(small_in, 96)
            nc.vector.tensor_scalar(bias_perm[:, 0, :].rearrange("p (a d g) -> p a d g", a=2, d=DH),
                                    bias_rows[:, 0, :].rearrange("p (g a d) -> p a d g", a=2, d=DH),
                                    SCALE, None, ALU.mult).then_inc(bias_permuted, 1)
            nc.vector.tensor_copy(bias_perm[:, 1, :].rearrange("p (a d g) -> p a d g", a=2, d=DH),
                                  bias_rows[:, 1, :].rearrange("p (g a d) -> p a d g", a=2, d=DH))\
                .then_inc(bias_permuted, 1)
            nc.vector.tensor_copy(bias_perm[:, 2, :], bias_rows[:, 2, :]).then_inc(bias_permuted, 1)
            nc.vector.tensor_scalar(mu_rest[:, :], mu[:, :], -1.0, 1.0, ALU.mult, ALU.add).then_inc(setup_dve, 1)
            dve.wait_ge(bias_turned, 3)
            nc.vector.tensor_copy(bias_cols[:, :], score[0][:, 0:3]).then_inc(bias_ready, 3)
            dve.wait_ge(bias_ready, 3)
            nc.vector.tensor_scalar(cbv_wide[:, :], one[:, :], bias_cols[:, 2:3], None, ALU.mult)\
                .then_inc(bias_wide, 1)
            dve.wait_ge(out_bias_mm, 1)
            nc.vector.tensor_tensor(out_bias[:, :], score[0][:, 0:P], cbo_wide[:, :], ALU.add).then_inc(setup_dve, 7)
            dve.wait_ge(mask_loaded, 16)
            nc.vector.tensor_scalar(mask_f[:, :], mask_in[:, :], MASK_WEIGHT, None, ALU.mult)\
                .then_inc(bias_permuted, 1)
            dve.wait_ge(bias_permuted, 4)
            nc.vector.tensor_copy(mask_parts[:, 0, :], mask_f[:, :]).then_inc(bias_permuted, 1)
            dve.wait_ge(bias_permuted, 5)
            nc.vector.tensor_tensor(mask_r[:, :], mask_f[:, :], mask_parts[:, 0, :], ALU.subtract)\
                .then_inc(bias_permuted, 1)
            dve.wait_ge(bias_permuted, 6)
            nc.vector.tensor_copy(mask_parts[:, 1, :], mask_r[:, :]).then_inc(setup_dve, 1)
            dve.wait_ge(setup_dve, 9)
            nc.vector.tensor_tensor(mask_parts[:, 2, :], mask_r[:, :], mask_parts[:, 1, :], ALU.subtract)\
                .then_inc(setup_dve, 1)
            dve.wait_ge(setup_dve, 10)

            def moments_of(n, src, q):
                for b in range(QB):
                    nc.vector.bn_stats(stats[n][:, b, :], src[:, b, :]).then_inc(ln_stats[n], 1)
                dve.wait_ge(ln_stats[n], QB * q + QB)
                if later(q):
                    dve.wait_ge(ln_rstd[n], q)
                mo, st = moments[n], stats[n]
                nc.vector.tensor_tensor(mo[:, 0], st[:, :, 1], st[:, :, 4], ALU.add).then_inc(ln_moments[n], 1)
                nc.vector.tensor_tensor(mo[:, 1], st[:, :, 1], st[:, :, 4], ALU.subtract).then_inc(ln_moments[n], 1)
                nc.vector.tensor_tensor(mo[:, 2], st[:, :, 2], st[:, :, 5], ALU.add).then_inc(ln_moments[n], 1)
                dve.wait_ge(ln_moments[n], 7 * q + 3)
                nc.vector.tensor_scalar(mo[:, 3], mo[:, 0], 0.5, None, ALU.mult).then_inc(ln_moments[n], 1)
                nc.vector.scalar_tensor_tensor(out=mo[:, 4], in0=mo[:, 1], scalar=0.25, in1=mo[:, 1],
                                               op0=ALU.mult, op1=ALU.mult).then_inc(ln_moments[n], 1)
                nc.vector.tensor_scalar(mo[:, 5], mo[:, 2], 1.0 / D, EPS, ALU.mult, ALU.add)\
                    .then_inc(ln_moments[n], 1)
                dve.wait_ge(ln_moments[n], 7 * q + 6)
                nc.vector.tensor_tensor(var_eps[n][:, :], mo[:, 4], mo[:, 5], ALU.add).then_inc(ln_moments[n], 1)

            def norm_of(n, src, q, turned):
                dve.wait_ge(ln_rstd[n], q + 1)
                if later(q):
                    dve.wait_ge(turned, q)
                for b in range(QB):
                    nc.vector.tensor_scalar(xn[n][:, b, :], src[:, b, :], moments[n][:, 3, b:b + 1],
                                            rstd[n][:, b:b + 1], ALU.subtract, ALU.mult).then_inc(ln_out[n], 1)

            def rest_of(src, parts, rest, hi, lo, left, q, bias=None):
                dve.wait_ge(hi, q + 1)
                if later(q):
                    dve.wait_ge(lo, q)
                if bias is None:
                    nc.vector.tensor_tensor(rest[:, :], src, parts[:, 0, :], ALU.subtract).then_inc(left, 1)
                else:
                    nc.vector.scalar_tensor_tensor(out=rest[:, :], in0=src, scalar=bias, in1=parts[:, 0, :],
                                                   op0=ALU.add, op1=ALU.subtract).then_inc(left, 1)

            def spread(values, src, rows, made, pv, ready, q):
                dve.wait_ge(made, q + 1)
                if later(q):
                    dve.wait_ge(pv, 8 * q)
                for b in range(QB):
                    nc.vector.tensor_copy(v_diag(values, b, rows),
                                          src[0:rows, D * b:D * b + D].rearrange("p (g i d) -> p g i d", i=4, d=DH))\
                        .then_inc(ready, 1)

            def normalize(b, q, pv, inv, inv_ready, att, ready, used):
                dve.wait_ge(pv, 8 * q + 2 * b + 2)
                if b >= 2:
                    dve.wait_ge(ready, 4 * q + b - 1)
                elif later(q):
                    dve.wait_ge(ready, 4 * q)
                nc.vector.reciprocal(inv[:, b % 2, :], sums[b % 2][:, 1, :]).then_inc(inv_ready, 1)
                dve.wait_ge(inv_ready, 4 * q + b + 1)
                if later(q) and b == 0:
                    dve.wait_ge(used, q)
                nc.vector.tensor_tensor(att[:, b, :], sums[b % 2][:, 0, :], inv[:, b % 2, :], ALU.mult)\
                    .then_inc(ready, 1)

            def step(s, body, back, head):
                u, n = s - 1, s + 1

                def max_self(k):
                    dve.wait_ge(s_made, 6 * s + k + 1)
                    if k == 0 and later(s):
                        dve.wait_ge(maxT_made, s)
                    bb, kind = 2 * (k // 3), k % 3
                    if kind < 2:
                        nc.vector.tensor_reduce(neg_max[:, 1, :, bb + kind],
                                                score[k % 2][:, :].rearrange("p (g k) -> p g k", g=G),
                                                AX_X, ALU.max, negate=True).then_inc(max_taken, 1)
                    else:
                        nc.vector.tensor_reduce(neg_max[:, 0, :, bb:bb + 2].rearrange("p g b -> p b g"),
                                                score[k % 2][:, :].rearrange("p (b g k) -> p b g k", b=2, g=G),
                                                AX_X, ALU.max, negate=True).then_inc(max_taken, 1)

                def max_cross(k):
                    b, a = k // 2, k % 2
                    dve.wait_ge(cs_made, 8 * u + k + 1)
                    if k == 0 and later(u):
                        dve.wait_ge(cmaxT_made, u)
                    src = score[k % 2][:, :].rearrange("p (n c) -> p n c", n=2)[:, :, 0:4 * TC]\
                        .rearrange("p n (i k) -> p n i k", k=TC)
                    nc.vector.tensor_reduce(cneg_max[:, a, :, b].rearrange("p (n i) -> p n i", n=2), src,
                                            AX_X, ALU.max, negate=True).then_inc(cmax_taken, 1)

                if body:
                    for k in range(6):
                        max_self(k)
                if back:
                    max_cross(0)
                    max_cross(1)
                if body:
                    dve.wait_ge(max_hi_ready, s + 1)
                    nc.vector.tensor_tensor(max_mid[:, :, :], max_f[:, :, :], max_hi[:, :, :], ALU.subtract)\
                        .then_inc(max_mid_ready, 1)
                if back:
                    for k in range(2, 8):
                        max_cross(k)
                if head:
                    dve.wait_ge(x_loaded, 16 * n + 16)
                    moments_of(0, x_in, n)
                    norm_of(0, x_in, n, xnT_made)
                if back:
                    dve.wait_ge(cmax_hi_ready, u + 1)
                    nc.vector.tensor_tensor(cmax_mid[:, :], cmax_f[:, :], cmax_hi[:, :], ALU.subtract)\
                        .then_inc(cmax_mid_ready, 1)
                if body:
                    for b in range(QB):
                        normalize(b, s, pv_done, den_inv, den_ready, attT, att_ready, o_made)
                    dve.wait_ge(o_made, s + 1)
                    if later(s):
                        dve.wait_ge(x1b_ready, s)
                        dve.wait_ge(ln_out[1], QB * s)
                    dve.wait_ge(x_kept, s + 1)
                    nc.vector.tensor_tensor(x1[:, :, :], proj[0][:, :].rearrange("p (b d) -> p b d", b=QB),
                                            x_res[:, :, :], ALU.add).then_inc(x1_ready, 1)
                    dve.wait_ge(x1_ready, s + 1)
                    moments_of(1, x1, s)
                if head:
                    rest_of(proj[0][:, :], q_parts, q_rest, q_hi, q_lo, q_left, n)
                    rest_of(proj[1][:, :], k_parts, k_rest, k_hi, k_lo, k_left, n)
                if body:
                    norm_of(1, x1, s, xcT_made)
                if head:
                    spread(v_heads, proj[0], P, v_made, pv_done, v_ready, n)
                if back:
                    for b in range(QB):
                        normalize(b, u, cpv_done, cden_inv, cden_ready, cattT, catt_ready, co_made)
                    dve.wait_ge(co_made, u + 1)
                    dve.wait_ge(x1b_ready, u + 1)
                    if later(u):
                        dve.wait_ge(y_ready, u)
                        dve.wait_ge(ln_out[2], QB * u)
                    nc.vector.tensor_tensor(x2[:, :, :], proj[1][:, :].rearrange("p (b d) -> p b d", b=QB),
                                            x1b[:, :, :], ALU.add).then_inc(x2_ready, 1)
                    dve.wait_ge(x2_ready, u + 1)
                    moments_of(2, x2, u)
                if body:
                    rest_of(proj[1][:, :], cq_parts, cq_rest, cq_hi, cq_lo, cq_left, s, bias_cols[:, 0:1])
                if back:
                    norm_of(2, x2, u, xeT_made)
                if body:
                    rest_of(proj[1][:, 0:NC], ck_parts, ck_rest, ck_hi, ck_lo, ck_left, s, bias_cols[:, 1:2])
                    spread(cv_heads, proj[0], TC, cv_made, cpv_done, cv_ready, s)
                if back:
                    dve.wait_ge(xeT_ready, u + 1)
                    if later(u):
                        dve.wait_ge(fr_made, u)
                        dve.wait_ge(mix_ready, 2 * u)
                    for m in (1, 0):
                        nc.vector.tensor_scalar(mix_a[:, m], xeT[:, :, 0:T], mu_rest[:, m:m + 1], None, ALU.mult)\
                            .then_inc(mix_part, 1)
                        dve.wait_ge(mix_part, 2 * u + (2 - m))
                        nc.vector.scalar_tensor_tensor(out=mixed[:, m], in0=xeT[:, :, 1:T + 1],
                                                       scalar=mu[:, m:m + 1], in1=mix_a[:, m],
                                                       op0=ALU.mult, op1=ALU.add).then_inc(mix_ready, 1)
                    dve.wait_ge(gate_tanh_ready, u + 1)
                    dve.wait_ge(fv_made, u + 1)
                    if later(u):
                        dve.wait_ge(y_ready, u)
                    nc.vector.scalar_tensor_tensor(out=y_gated[:, :], in0=gate_tanh[:, :], scalar=1.0,
                                                   in1=proj[0][:, :], op0=ALU.add, op1=ALU.mult)\
                        .then_inc(y_gated_ready, 1)

            def v_diag(heads, b, rows):
                flat = heads[0:rows, b].rearrange("p (g i) c -> p g (i c)", i=4)
                skew = bass.AP(tensor=flat.tensor, offset=flat.offset,
                               ap=[list(flat.ap[0]), [128, 4], [40, 4], [1, DH]])
                return skew

            schedule(dve, step)

        @block.tensor
        def _(pe):
            pe.wait_ge(ident_made, 1)
            pe.wait_ge(w_in, 176)
            for n in (CQ, CK, CV, CO, FR, FK, FV):
                j = n - CQ
                last = nc.tensor.transpose(proj[j // 4][:, P * (j % 4):P * (j % 4) + P], w_raw[:, n, :], ident[:, :])
                if n in (CO, FV):
                    last.then_inc(w_turned, 1)
            pe.wait_ge(bias_permuted, 3)
            pe.wait_ge(consts_made, 9)
            for n in range(3):
                nc.tensor.matmul(score[0][:, n:n + 1], bias_perm[0:1, n, :], one[0:1, 0:1], start=True, stop=True)\
                    .then_inc(bias_turned, 1)
            pe.wait_ge(bias_wide, 1)
            pe.wait_ge(w_ready, 11)
            nc.tensor.matmul(score[0][:, 0:P], cbv_wide[:, :], wT[:, CO, :], start=True, stop=True)\
                .then_inc(out_bias_mm, 1)
            pe.wait_ge(consts_made, 23)
            pe.wait_ge(setup_dve, 8)

            def turn(dst, src, rows):
                for b in range(QB):
                    last = nc.tensor.transpose(dst[:, rows * b:rows * b + rows], src[0:rows, b, :],
                                               ident[0:rows, 0:rows])
                return last

            def score_max_self(k):
                bb, kind = 2 * (k // 3), k % 3
                dst = score[k % 2]
                if kind < 2:
                    b = bb + kind
                    for n in range(2):
                        nc.tensor.matmul(dst[:, 512 * n:512 * n + 512], pick_hi[:, :, :], band[:, :, :],
                                         start=True, stop=False)
                    for g in range(G):
                        for a in range(2):
                            last = nc.tensor.matmul(dst[HALF * a:HALF * a + HALF, T * g:T * g + T],
                                                    q_stack[0:NSTACK, a, g, b, HALF:T],
                                                    k_stack[0:NSTACK, g, b, :], start=False, stop=(g % 4 == 3))
                else:
                    for n in range(2):
                        nc.tensor.matmul(dst[:, 512 * n:512 * n + 512], pick_lo[:, :, :], band_lo[:, :, :],
                                         start=True, stop=False)
                        for g in range(G):
                            c = 512 * n + HALF * g
                            for a in range(2):
                                last = nc.tensor.matmul(dst[HALF * a:HALF * a + HALF, c:c + HALF],
                                                        q_stack[0:NSTACK, a, g, bb + n, 0:HALF],
                                                        k_stack[0:NSTACK, g, bb + n, 0:HALF],
                                                        start=False, stop=(g == G - 1))
                last.then_inc(s_made, 1)

            def attend(k, probs_in, values, ready, ready_value, done):
                b, j = k // 2, k % 2
                pe.wait_ge(ready, ready_value)
                dst = sums[b % 2]
                for a in range(2):
                    for g in range(4):
                        nc.tensor.matmul(dst[32 * g:32 * g + 32, 0, :], values[:, b, 4 * g + 2 * j + a, :],
                                         probs_in[:, k % 2, g, a, :], start=(j == 0 and a == 0),
                                         stop=(j == 1 and a == 1), tile_position=(0, 32 * g),
                                         skip_group_check=True)
                for a in range(2):
                    for g in range(4):
                        last = nc.tensor.matmul(dst[32 * g:32 * g + 32, 1, :], head_ones[:, 2 * j + a, :],
                                                probs_in[:, k % 2, g, a, :], start=False,
                                                stop=(j == 1 and a == 1), tile_position=(0, 32 * g),
                                                skip_group_check=True)
                last.then_inc(done, 1)

            def project_out(att, w, ready, q, dst, made):
                for b in range(QB):
                    pe.wait_ge(ready, QB * q + b + 1)
                    last = nc.tensor.matmul(dst[:, D * b:D * b + D], att[:, b, :], wT[:, w, :],
                                            start=True, stop=True)
                last.then_inc(made, 1)

            def step(s, body, back, head):
                u, n = s - 1, s + 1

                def self_slot(k):
                    if k >= 2:
                        pe.wait_ge(max_taken, 6 * s + k - 1)
                    elif back and later(u):
                        pe.wait_ge(cexp_done, 8 * (u - 1) + 7 + k)
                    elif later(s):
                        pe.wait_ge(exp_done, 8 * (s - 1) + 7 + k)
                    score_max_self(k)

                def cross_slot(k):
                    b, a = k // 2, k % 2
                    if k >= 2:
                        pe.wait_ge(cmax_taken, 8 * u + k - 1)
                    elif body:
                        pe.wait_ge(max_taken, 6 * s + 5 + k)
                    else:
                        pe.wait_ge(cexp_done, 8 * (u - 1) + 7 + k)
                    for g in range(G):
                        c = 512 * (g // 4) + TC * (g % 4)
                        last = nc.tensor.matmul(score[k % 2][:, c:c + TC], cq_stack[0:SHIFT_CROSS, a, g, b, :],
                                                ck_stack[0:SHIFT_CROSS, g, b, :], start=True, stop=True)
                    last.then_inc(cs_made, 1)

                def self_scores(k):
                    b, j = k // 2, k % 2
                    if k >= 2:
                        pe.wait_ge(exp_done, 8 * s + k - 1)
                    elif back:
                        pe.wait_ge(cmax_taken, 8 * u + 7 + k)
                    else:
                        pe.wait_ge(max_taken, 6 * s + 5 + k)
                    for m in range(2):
                        nc.tensor.matmul(score[k % 2][:, 512 * m:512 * m + 512], band[:, 0, :], ident_bf[:, :, :],
                                         start=True, stop=False)
                    for i in range(4):
                        g = 2 * i + j
                        last = nc.tensor.matmul(score[k % 2][:, 256 * i:256 * i + 256], k_stack[:, g, b, :],
                                                q_stack[:, :, g, b, :], start=False, stop=(i % 2 == 1))
                    last.then_inc(sT_made, 1)

                def attend_self(k):
                    b = k // 2
                    if k % 2 == 0:
                        if b >= 2:
                            pe.wait_ge(att_ready, 4 * s + b - 1)
                        elif back and later(u):
                            pe.wait_ge(catt_ready, 4 * (u - 1) + 3 + b)
                        elif later(s):
                            pe.wait_ge(att_ready, 4 * (s - 1) + 3 + b)
                    attend(k, probs, v_heads, exp_done, 8 * s + k + 1, pv_done)

                def cross_scores(k):
                    b, j = k // 2, k % 2
                    if k >= 2:
                        pe.wait_ge(cexp_done, 8 * u + k - 1)
                    elif body:
                        pe.wait_ge(exp_done, 8 * s + 7 + k)
                    else:
                        pe.wait_ge(cmax_taken, 8 * u + 7 + k)
                    for i in range(4):
                        g = 2 * i + j
                        last = nc.tensor.matmul(score[k % 2][0:TC, 256 * i:256 * i + 256], ck_stack[:, g, b, :],
                                                cq_stack[:, :, g, b, :], start=True, stop=True)
                    last.then_inc(csT_made, 1)

                def attend_cross(k):
                    b = k // 2
                    if k % 2 == 0:
                        if b >= 2:
                            pe.wait_ge(catt_ready, 4 * u + b - 1)
                        elif body:
                            pe.wait_ge(att_ready, 4 * s + 3 + b)
                        else:
                            pe.wait_ge(catt_ready, 4 * (u - 1) + 3 + b)
                    attend(k, cprobs, cv_heads, cexp_done, 8 * u + k + 1, cpv_done)

                if body:
                    pe.wait_ge(q_stacked, 96 * s + 96)
                    pe.wait_ge(k_stacked, 192 * s + 192)
                    for k in range(6):
                        self_slot(k)
                if back:
                    pe.wait_ge(cq_stacked, 96 * u + 96)
                    pe.wait_ge(ck_stacked, 192 * u + 192)
                    pe.wait_ge(cbias_in, 16 * u + 16)
                    cross_slot(0)
                    cross_slot(1)
                if body:
                    pe.wait_ge(max_taken, 6 * s + 6)
                    if back and later(u):
                        pe.wait_ge(y_gated_ready, u)
                    pe.wait_ge(v_ready, QB * s + QB)
                    if later(s):
                        pe.wait_ge(cv_ready, QB * s)
                    nc.tensor.transpose(proj[0][:, 0:T], neg_max[:, :, :, :], ident[:, :]).then_inc(maxT_made, 1)
                if back:
                    for k in range(2, 8):
                        cross_slot(k)
                if body:
                    pe.wait_ge(shift_in, 64 * s + 64)
                    self_scores(0)
                    self_scores(1)
                if back:
                    pe.wait_ge(cmax_taken, 8 * u + 8)
                    pe.wait_ge(ck_left, u + 1)
                    if later(u):
                        pe.wait_ge(gate_tanh_ready, u)
                    nc.tensor.transpose(proj[1][:, 0:T], cneg_max[:, :, :, :], ident[:, :]).then_inc(cmaxT_made, 1)
                if body:
                    for k in range(8):
                        attend_self(k)
                        if k + 2 < 8:
                            self_scores(k + 2)
                    pe.wait_ge(max_f_ready, 2 * s + 2)
                    project_out(attT, SO, att_ready, s, proj[0], o_made)
                if head:
                    pe.wait_ge(ln_out[0], QB * n + QB)
                    if back:
                        pe.wait_ge(cmax_f_ready, u + 1)
                    elif body:
                        pe.wait_ge(k_left, n)
                    turn(proj[1], xn[0], T).then_inc(xnT_made, 1)
                    pe.wait_ge(xnT_ready, n + 1)
                    if body:
                        pe.wait_ge(x1_ready, s + 1)
                    nc.tensor.matmul(proj[0][:, :], wT[:, SQ, :], xnT[:, :], start=True, stop=True)\
                        .then_inc(q_made, 1)
                    nc.tensor.matmul(proj[1][:, :], wT[:, SK, :], xnT[:, :], start=True, stop=True)\
                        .then_inc(k_made, 1)
                    pe.wait_ge(q_left, n + 1)
                    for b in range(QB):
                        last = nc.tensor.matmul(proj[0][:, D * b:D * b + D], xnT[:, T * b:T * b + T], wT[:, SV, :],
                                                start=True, stop=True)
                    last.then_inc(v_made, 1)
                if back:
                    pe.wait_ge(cshift_in, 64 * u + 64)
                    pe.wait_ge(cv_ready, QB * u + QB)
                    cross_scores(0)
                    cross_scores(1)
                    for k in range(8):
                        attend_cross(k)
                        if k + 2 < 8:
                            cross_scores(k + 2)
                    pe.wait_ge(cmax_f_ready, u + 1)
                    if head:
                        pe.wait_ge(k_left, n + 1)
                    project_out(cattT, CO, catt_ready, u, proj[1], co_made)
                if body:
                    pe.wait_ge(ln_out[1], QB * s + QB)
                    pe.wait_ge(x1_ready, s + 1)
                    if head:
                        pe.wait_ge(v_ready, QB * n + QB)
                    turn(proj[0], xn[1], T).then_inc(xcT_made, 1)
                    pe.wait_ge(xcT_ready, s + 1)
                    if back:
                        pe.wait_ge(x2_ready, u + 1)
                    else:
                        pe.wait_ge(k_left, n + 1)
                    nc.tensor.matmul(proj[1][:, :], wT[:, CQ, :], xcT[:, :], start=True, stop=True)\
                        .then_inc(cq_made, 1)
                    pe.wait_ge(ctx_loaded, 16 * s + 16)
                    turn(proj[0], ctx_in, TC).then_inc(ctxT_made, 1)
                    pe.wait_ge(ctxT_ready, s + 1)
                    pe.wait_ge(cq_left, s + 1)
                    nc.tensor.matmul(proj[1][:, 0:NC], wT[:, CK, :], ctxT[:, :], start=True, stop=True)\
                        .then_inc(ck_made, 1)
                    for b in range(QB):
                        last = nc.tensor.matmul(proj[0][0:TC, D * b:D * b + D], ctxT[:, TC * b:TC * b + TC],
                                                wT[:, CV, :], start=True, stop=True)
                    last.then_inc(cv_made, 1)
                if back:
                    pe.wait_ge(ln_out[2], QB * u + QB)
                    if body:
                        pe.wait_ge(ck_left, s + 1)
                    else:
                        pe.wait_ge(x2_ready, u + 1)
                    turn(proj[1], xn[2], T).then_inc(xeT_made, 1)
                    pe.wait_ge(mix_ready, 2 * u + 1)
                    if body:
                        pe.wait_ge(cv_ready, QB * s + QB)
                    nc.tensor.matmul(proj[0][:, :], wT[:, FK, :], mixed[:, 1].rearrange("p b t -> p (b t)"),
                                     start=True, stop=True).then_inc(fk_made, 1)
                    pe.wait_ge(mix_ready, 2 * u + 2)
                    pe.wait_ge(xeT_ready, u + 1)
                    for b in range(QB):
                        last = nc.tensor.matmul(proj[1][:, D * b:D * b + D], mixed[:, 0, b, :], wT[:, FR, :],
                                                start=True, stop=True)
                    last.then_inc(fr_made, 1)
                    pe.wait_ge(relu_ready, u + 1)
                    pe.wait_ge(k_act_ready, u + 1)
                    for b in range(QB):
                        last = nc.tensor.matmul(proj[0][:, D * b:D * b + D], k_act[:, b, :], wT[:, FV, :],
                                                start=True, stop=True)
                    last.then_inc(fv_made, 1)

            schedule(pe, step)


_INS = ['x', 'ctx_1024', 'mask_BxS2_ik1', 'L0_attn_Wq', 'L0_attn_Wk', 'L0_attn_Wv', 'L0_attn_Wo',
        'L0_xattn_Wq', 'L0_xattn_bq', 'L0_xattn_Wk', 'L0_xattn_bk', 'L0_xattn_Wv', 'L0_xattn_bv',
        'L0_xattn_Wo', 'L0_xattn_bo', 'L0_ffn_W_r', 'L0_ffn_W_k', 'L0_ffn_W_v', 'L0_ffn_mu_r', 'L0_ffn_mu_k']
_OUTS = [((BATCH, T, D), 'float32')]


def kernel(**inputs):
    import numpy as _np
    import concourse.bacc as _bacc
    from concourse import mybir as _mybir
    from concourse.bass_utils import run_bass_kernel_spmd as _run

    nc = _bacc.Bacc("TRN2", target_bir_lowering=False, num_devices=1)
    arrays, args = {}, []
    for name in _INS:
        a = _np.ascontiguousarray(inputs[name])
        arrays[f"in_{name}_dram"] = a
        args.append(nc.dram_tensor(f"in_{name}_dram", a.shape, _mybir.dt.from_np(a.dtype), kind="ExternalInput").ap())
    for i, (shape, dtype) in enumerate(_OUTS):
        dt = _mybir.dt.from_np(_np.dtype(dtype))
        args.append(nc.dram_tensor(f"out_{i}_dram", shape, dt, kind="ExternalOutput").ap())
    decoder_layer(nc, *args)
    r = _run(nc, [arrays], core_ids=[0])
    got = tuple(r.results[0][f"out_{i}_dram"] for i in range(len(_OUTS)))
    return got[0]
```

```python
from contextlib import ExitStack

import concourse.bass as bass
from concourse import mybir

F32 = mybir.dt.float32
BF16 = mybir.dt.bfloat16
I32 = mybir.dt.int32
ALU = mybir.AluOpType
ACT = mybir.ActivationFunctionType
AX_X = mybir.AxisListType.X

P = 128
BATCH, T, D = 64, 128, 128
TC = 77
H, DH = 16, 8
G = H // 2
QB = 4
NQ = BATCH // QB
NT, NC = QB * T, QB * TC
WIN = 64
HALF = T // 2
SCALE = float(DH) ** -0.5
EPS = 1e-5
MASKED = -1e30
MASK_WEIGHT = -100.0

QPART = (0, 1, 2, 0, 1, 0)
KPART = (0, 0, 0, 1, 1, 2)
NSTACK = 2 * len(QPART) * DH
SHIFT_SELF = NSTACK
BIAS_CROSS = NSTACK
SHIFT_CROSS = NSTACK + 3
MC_SLOT = (1, 1, 1, 1, 1, 1, 1, 0)
ST_SLOT = (0, 1, 0, 1, 0, 0, 0, 0)


def decoder_layer(nc, x, ctx, mask, wq, wk, wv, wo, cwq, cbq, cwk, cbk, cwv, cbv, cwo, cbo,
                  fwr, fwk, fwv, mu_r, mu_k, out):
    x_quads = x.rearrange("(n b) t d -> n t b d", b=QB)
    out_quads = out.rearrange("(n b) t d -> n t b d", b=QB)
    ctx_quads = ctx.rearrange("(n b) s d -> n s b d", b=QB)

    def scratch(name, shape):
        return nc.dram_tensor(name, shape, BF16).ap()

    q_scr = scratch("q_scr", [2, 3, DH, G, NT])
    k_scr = scratch("k_scr", [2, len(KPART), DH, G, NT])
    cq_scr = scratch("cq_scr", [2, 3, DH, G, NT])
    ck_scr = scratch("ck_scr", [2, len(KPART), DH, G, NC])
    bias_scr = scratch("bias_scr", [3, NQ, G, NC])
    bias_quads = bias_scr.rearrange("c n g s -> n c (g s)")

    with ExitStack() as stack:
        def sb(name, shape, dt=F32):
            return stack.enter_context(nc.sbuf_tensor(name, shape, dt))

        def sem(name):
            return stack.enter_context(nc.semaphore(name))

        ident = sb("ident", [P, P])
        ident_bf = sb("ident_bf", [P, 4, P], BF16)
        band = sb("band", [P, 4, P], BF16)
        band_lo = sb("band_lo", [P, G, HALF], BF16)
        pick_hi = sb("pick_hi", [P, 2, HALF], BF16)
        pick_lo = sb("pick_lo", [P, 2, HALF], BF16)
        head_ones = sb("head_ones", [P, 4, 32])
        one = sb("one", [P, P])
        neg_half = sb("neg_half", [P, QB])
        w_raw = sb("w_raw", [P, 11, P])
        wT = sb("wT", [P, 11, P])
        (SQ, SK, SV, SO, CQ, CK, CV, CO, FR, FK, FV) = range(11)
        bias_rows = sb("bias_rows", [1, 3, P])
        bias_perm = sb("bias_perm", [1, 3, P])
        bias_cols = sb("bias_cols", [P, 3])
        cbv_wide = sb("cbv_wide", [P, P])
        cbo_wide = sb("cbo_wide", [P, P])
        out_bias = sb("out_bias", [P, P])
        mu = sb("mu", [P, 2])
        mu_rest = sb("mu_rest", [P, 2])
        mask_in = sb("mask_in", [NQ, NC], I32)
        mask_f = sb("mask_f", [NQ, NC])
        mask_r = sb("mask_r", [NQ, NC])
        mask_parts = sb("mask_parts", [NQ, 3, NC], BF16)

        x_in = sb("x_in", [P, QB, D])
        x_res = sb("x_res", [P, QB, D])
        stats = [sb(f"stats{n}", [P, QB, 6]) for n in range(3)]
        moments = [sb(f"moments{n}", [P, 6, QB]) for n in range(3)]
        var_eps = [sb(f"var_eps{n}", [P, QB]) for n in range(3)]
        rstd = [sb(f"rstd{n}", [P, QB]) for n in range(3)]
        xn = [sb(f"xn{n}", [P, QB, D]) for n in range(3)]
        xnT = sb("xnT", [P, NT])
        q_parts = sb("q_parts", [P, 3, NT], BF16)
        k_parts = sb("k_parts", [P, 3, NT], BF16)
        q_rest = sb("q_rest", [P, NT])
        k_rest = sb("k_rest", [P, NT])
        q_stack = sb("q_stack", [P, 2, G, QB, T], BF16)
        k_stack = sb("k_stack", [P, G, QB, T], BF16)
        v_heads = sb("v_heads", [P, QB, H, 32])
        neg_max = sb("neg_max", [P, 4, G, QB])
        max_f = sb("max_f", [G * QB, 2, T])
        max_hi = sb("max_hi", [G * QB, 2, T], BF16)
        max_mid = sb("max_mid", [G * QB, 2, T], BF16)
        probs = sb("probs", [P, 3, 4, 2, T])
        den_inv = sb("den_inv", [P, 2, T])
        attT = sb("attT", [P, QB, T])
        x1 = sb("x1", [P, QB, D])
        x1b = sb("x1b", [P, QB, D])

        ctx_in = sb("ctx_in", [TC, QB, D])
        ctxT = sb("ctxT", [P, NC])
        xcT = sb("xcT", [P, NT])
        cq_parts = sb("cq_parts", [P, 3, NT], BF16)
        ck_parts = sb("ck_parts", [P, 3, NC], BF16)
        cq_rest = sb("cq_rest", [P, NT])
        ck_rest = sb("ck_rest", [P, NC])
        cq_stack = sb("cq_stack", [P, 2, G, QB, T], BF16)
        ck_stack = sb("ck_stack", [P, G, QB, TC], BF16)
        cv_heads = sb("cv_heads", [P, QB, H, 32])
        cneg_max = sb("cneg_max", [P, 4, G, QB])
        cmax_f = sb("cmax_f", [2 * G * QB, T])
        cmax_hi = sb("cmax_hi", [2 * G * QB, T], BF16)
        cmax_mid = sb("cmax_mid", [2 * G * QB, T], BF16)
        cprobs = sb("cprobs", [P, 2, 4, 2, T])
        cden_inv = sb("cden_inv", [P, 2, T])
        cattT = sb("cattT", [P, QB, T])
        x2 = sb("x2", [P, QB, D])
        mix_a = sb("mix_a", [P, 2, QB, T])
        mixed = sb("mixed", [P, 2, QB, T])
        k_relu = sb("k_relu", [P, NT])
        k_act = sb("k_act", [P, QB, T])
        gate_tanh = sb("gate_tanh", [P, NT])
        y_gated = sb("y_gated", [P, NT])
        y_out = sb("y_out", [P, QB, D])

        score = [stack.enter_context(nc.psum_tensor(f"score{n}", [P, 1024], F32)) for n in range(2)]
        sums = [stack.enter_context(nc.psum_tensor(f"sums{n}", [P, 4, T], F32)) for n in range(2)]
        proj = [stack.enter_context(nc.psum_tensor(f"proj{n}", [P, 512], F32)) for n in range(2)]

        w_in = sem("w_in")
        small_in = sem("small_in")
        mask_loaded = sem("mask_loaded")
        ident_zero = sem("ident_zero")
        ident_made = sem("ident_made")
        consts_made = sem("consts_made")
        zeros_made = sem("zeros_made")
        cross_zeros = sem("cross_zeros")
        pad_zeros = sem("pad_zeros")
        ones_rows = sem("ones_rows")
        w_turned = sem("w_turned")
        w_ready = sem("w_ready")
        bias_permuted = sem("bias_permuted")
        bias_turned = sem("bias_turned")
        bias_ready = sem("bias_ready")
        bias_wide = sem("bias_wide")
        out_bias_mm = sem("out_bias_mm")
        setup_dve = sem("setup_dve")
        bias_stored = sem("bias_stored")

        x_loaded = sem("x_loaded")
        x_kept = sem("x_kept")
        ln_stats = [sem(f"ln_stats{n}") for n in range(3)]
        ln_moments = [sem(f"ln_moments{n}") for n in range(3)]
        ln_rstd = [sem(f"ln_rstd{n}") for n in range(3)]
        ln_out = [sem(f"ln_out{n}") for n in range(3)]
        xnT_made = sem("xnT_made")
        xnT_ready = sem("xnT_ready")
        q_made = sem("q_made")
        q_hi = sem("q_hi")
        q_left = sem("q_left")
        q_mid = sem("q_mid")
        q_lo = sem("q_lo")
        k_made = sem("k_made")
        k_hi = sem("k_hi")
        k_left = sem("k_left")
        k_mid = sem("k_mid")
        k_lo = sem("k_lo")
        v_made = sem("v_made")
        v_ready = sem("v_ready")
        q_stored = sem("q_stored")
        k_stored = sem("k_stored")
        q_stacked = sem("q_stacked")
        k_stacked = sem("k_stacked")
        s_made = sem("s_made")
        max_taken = sem("max_taken")
        maxT_made = sem("maxT_made")
        max_f_ready = sem("max_f_ready")
        max_hi_ready = sem("max_hi_ready")
        max_mid_ready = sem("max_mid_ready")
        shift_in = sem("shift_in")
        sT_made = sem("sT_made")
        exp_done = sem("exp_done")
        pv_done = sem("pv_done")
        den_ready = sem("den_ready")
        att_ready = sem("att_ready")
        o_made = sem("o_made")
        x1_ready = sem("x1_ready")
        x1b_ready = sem("x1b_ready")

        ctx_loaded = sem("ctx_loaded")
        ctxT_made = sem("ctxT_made")
        ctxT_ready = sem("ctxT_ready")
        cbias_in = sem("cbias_in")
        xcT_made = sem("xcT_made")
        xcT_ready = sem("xcT_ready")
        cq_made = sem("cq_made")
        cq_hi = sem("cq_hi")
        cq_left = sem("cq_left")
        cq_mid = sem("cq_mid")
        cq_lo = sem("cq_lo")
        ck_made = sem("ck_made")
        ck_hi = sem("ck_hi")
        ck_left = sem("ck_left")
        ck_mid = sem("ck_mid")
        ck_lo = sem("ck_lo")
        cv_made = sem("cv_made")
        cv_ready = sem("cv_ready")
        cq_stored = sem("cq_stored")
        ck_stored = sem("ck_stored")
        cq_stacked = sem("cq_stacked")
        ck_stacked = sem("ck_stacked")
        cs_made = sem("cs_made")
        cmax_taken = sem("cmax_taken")
        cmaxT_made = sem("cmaxT_made")
        cmax_f_ready = sem("cmax_f_ready")
        cmax_hi_ready = sem("cmax_hi_ready")
        cmax_mid_ready = sem("cmax_mid_ready")
        cshift_in = sem("cshift_in")
        csT_made = sem("csT_made")
        cexp_done = sem("cexp_done")
        cpv_done = sem("cpv_done")
        cden_ready = sem("cden_ready")
        catt_ready = sem("catt_ready")
        co_made = sem("co_made")
        x2_ready = sem("x2_ready")
        xeT_made = sem("xeT_made")
        mix_part = sem("mix_part")
        mix_ready = sem("mix_ready")
        fk_made = sem("fk_made")
        relu_ready = sem("relu_ready")
        k_act_ready = sem("k_act_ready")
        fr_made = sem("fr_made")
        gate_tanh_ready = sem("gate_tanh_ready")
        fv_made = sem("fv_made")
        y_gated_ready = sem("y_gated_ready")
        y_ready = sem("y_ready")
        y_stored = sem("y_stored")

        block = stack.enter_context(nc.Block())

        def schedule(eng, step):
            step(-1, False, False, False, True)
            step(0, False, False, True, True)
            step(1, False, True, True, True)
            step(2, True, True, True, True)
            with eng.Fori(3, NQ - 1) as s:
                step(s, True, True, True, True)
            step(NQ - 1, True, True, True, False)
            step(NQ, True, True, False, False)
            step(NQ + 1, True, False, False, False)

        def later(q):
            return not isinstance(q, int) or q > 0

        @block.sync
        def _(sp):
            sp.dma_start(x_in[:, :, :], x_quads[0]).then_inc(x_loaded, 16)
            for n, w in enumerate((wq, wk, wv, wo, cwq, cwk, cwv, cwo, fwr, fwk, fwv)):
                sp.dma_start(w_raw[:, n, :], w).then_inc(w_in, 16)
            for n, b in enumerate((cbq, cbk, cbv)):
                sp.dma_start(bias_rows[:, n, :], b.rearrange("(o d) -> o d", o=1)).then_inc(small_in, 16)
            for n, m in enumerate((mu_r, mu_k)):
                sp.dma_start(mu[:, n:n + 1], m.rearrange("(d o) -> d o", o=1)).then_inc(small_in, 16)
            sp.dma_start(cbo_wide[:, :], cbo.partition_broadcast(P)).then_inc(small_in, 16)
            sp.dma_start(mask_in[:, :], mask.rearrange("(n b) s -> n (b s)", b=QB)).then_inc(mask_loaded, 16)

            def cross_constants():
                sp.wait_ge(cross_zeros, 2)
                for r in range(4):
                    sp.dma_start(cq_stack[BIAS_CROSS:BIAS_CROSS + 3, r // 2, 4 * (r % 2):4 * (r % 2) + 4]
                                 .rearrange("p g b q -> p (g b q)"),
                                 ck_stack[BIAS_CROSS:BIAS_CROSS + 3]
                                 .rearrange("p g b k -> p (g b k)")[:, 0:2048]).then_inc(ones_rows, 16)
                sp.wait_ge(setup_dve, 10)
                for g in range(G):
                    sp.dma_start(bias_scr[:, :, g, :].rearrange("c n s -> n c s"), mask_parts[:, :, :])\
                        .then_inc(bias_stored, 16)

            def store_parts(parts, scr, stored):
                for a in range(2):
                    sp.dma_start(scr[a].rearrange("p d g t -> (d g) p t"),
                                 parts[HALF * a:HALF * a + HALF]).then_inc(stored, 16)

            def stack_queries(scr, dst, stacked):
                rows = dst.rearrange("p a g b q -> p a (g b q)")
                for a in range(2):
                    for c, n in ((0, 3), (3, 2), (5, 1)):
                        r = 48 * a + DH * c
                        sp.dma_start(rows[r:r + DH * n, a, :],
                                     scr[a, 0:n].rearrange("p d g t -> (p d) (g t)")).then_inc(stacked, 16)

            def store_key_rows(parts, scr, stored):
                for a in range(2):
                    for c, part in enumerate(KPART):
                        if part == 0 and c or part == 1 and KPART[c - 1] == 1:
                            continue
                        n = KPART.count(part)
                        sp.dma_start(scr[a, c:c + n].rearrange("c d g t -> (d g) c t"),
                                     parts[HALF * a:HALF * a + HALF, part:part + 1, :]
                                     .to_broadcast([HALF, n, parts.shape[2]])).then_inc(stored, 16)

            def stack_keys(scr, dst, stacked):
                rows = dst.rearrange("p g b k -> p (g b k)")
                for a in range(2):
                    sp.dma_start(rows[48 * a:48 * a + 48, :],
                                 scr[a].rearrange("c d g t -> (c d) (g t)")).then_inc(stacked, 16)

            def step(s, tail, back, body, head):
                t, u, n = s - 2, s - 1, s + 1
                if head and body:
                    sp.wait_ge(ln_out[0], QB * n)
                    sp.wait_ge(x_kept, n)
                    sp.dma_start(x_in[:, :, :], x_quads[n] if isinstance(s, int) else x_quads[1:][s])\
                        .then_inc(x_loaded, 16)
                if back:
                    if later(u):
                        sp.wait_ge(csT_made, 8 * u)
                    else:
                        sp.wait_ge(ones_rows, 64)
                        sp.wait_ge(bias_stored, 16 * G)
                    sp.dma_start(ck_stack[BIAS_CROSS:BIAS_CROSS + 3].rearrange("p g b k -> p (g b k)"),
                                 bias_quads[u]).then_inc(cbias_in, 16)
                    sp.wait_ge(ck_stored, 96 * u + 96)
                    stack_keys(ck_scr, ck_stack[:, :, :, :], ck_stacked)
                    sp.wait_ge(cq_stored, 32 * u + 32)
                    stack_queries(cq_scr, cq_stack[:, :, :, :, :], cq_stacked)
                if body:
                    if later(s):
                        sp.wait_ge(ctxT_made, s)
                    sp.dma_start(ctx_in[:, :, :], ctx_quads[s]).then_inc(ctx_loaded, 16)
                    if not later(s):
                        cross_constants()
                if head:
                    sp.wait_ge(k_lo, n + 1)
                    store_key_rows(k_parts[:, :, :], k_scr, k_stored)
                if tail:
                    sp.wait_ge(y_ready, t + 1)
                    sp.dma_start(out_quads[t], y_out[:, :, :]).then_inc(y_stored, 16)
                if back:
                    for part, src, ready in ((0, cmax_hi, cmax_hi_ready), (1, cmax_mid, cmax_mid_ready)):
                        sp.wait_ge(ready, u + 1)
                        for a in range(2):
                            r = SHIFT_CROSS + 2 * a + part
                            sp.dma_start(cq_stack[r:r + 1, a].rearrange("o g b q -> o (g b) q"),
                                         src[32 * a:32 * a + 32, :]).then_inc(cshift_in, 16)
                if head:
                    sp.wait_ge(q_lo, n + 1)
                    store_parts(q_parts[:, :, :], q_scr, q_stored)
                    if body:
                        sp.wait_ge(sT_made, 8 * s + 8)
                    else:
                        sp.wait_ge(zeros_made, 2)
                    sp.wait_ge(k_stored, 96 * n + 96)
                    stack_keys(k_scr, k_stack[:, :, :, :], k_stacked)
                    sp.wait_ge(q_stored, 32 * n + 32)
                    stack_queries(q_scr, q_stack[:, :, :, :, :], q_stacked)
                if body:
                    sp.wait_ge(ck_lo, s + 1)
                    store_key_rows(ck_parts[:, :, :], ck_scr, ck_stored)
                if head:
                    for part, src, ready in ((0, max_hi, max_hi_ready), (1, max_mid, max_mid_ready)):
                        sp.wait_ge(ready, n + 1)
                        for a in range(2):
                            r = SHIFT_SELF + 2 * a + part
                            sp.dma_start(q_stack[r:r + 1, a].rearrange("o g b q -> o (g b) q"),
                                         src[:, a, :]).then_inc(shift_in, 16)
                if body:
                    sp.wait_ge(cq_lo, s + 1)
                    store_parts(cq_parts[:, :, :], cq_scr, cq_stored)

            schedule(sp, step)
            sp.wait_ge(y_stored, 16 * NQ)

        @block.gpsimd
        def _(pool):
            nc.gpsimd.memset(ident[:, :], 0.0).then_inc(ident_zero, 1)
            nc.gpsimd.memset(band[:, :, :], 0.0).then_inc(ident_zero, 1)
            pool.wait_ge(ident_zero, 2)
            nc.gpsimd.affine_select(out=ident[:, :], in_=ident[:, :], compare_op=ALU.not_equal, fill=1.0,
                                    base=0, pattern=[[-1, P]], channel_multiplier=1).then_inc(ident_made, 1)
            nc.gpsimd.affine_select(out=band[:, :, :], in_=band[:, :, :], compare_op=ALU.is_ge, fill=MASKED,
                                    base=0, pattern=[[0, 4], [-1, P]], channel_multiplier=1)\
                .then_inc(ident_made, 1)
            pool.wait_ge(ident_made, 2)
            nc.gpsimd.affine_select(out=band[:, :, :], in_=band[:, :, :], compare_op=ALU.is_ge, fill=MASKED,
                                    base=WIN - 1, pattern=[[0, 4], [1, P]], channel_multiplier=-1)\
                .then_inc(ident_made, 1)

            for zeros in (v_heads[:, :, :, :], cv_heads[:, :, :, :], mix_a[:, :, :, :], cprobs[:, :, :, :, :]):
                nc.gpsimd.memset(zeros, 0.0).then_inc(pad_zeros, 1)
            nc.gpsimd.memset(k_stack[:, :, :, :], 1.0).then_inc(zeros_made, 1)

            def rstd_of(n, q):
                pool.wait_ge(ln_moments[n], 7 * q + 7)
                pool.wait_ge(ln_out[n], QB * q)
                nc.gpsimd.tensor_tensor(rstd[n][:, :], var_eps[n][:, :], neg_half[:, :], ALU.pow)\
                    .then_inc(ln_rstd[n], 1)

            def low_part(parts, rest, left, mid, lo, stored, count, q):
                if later(q):
                    pool.wait_ge(stored, count * q)
                pool.wait_ge(left, q + 1)
                pool.wait_ge(mid, q + 1)
                nc.gpsimd.tensor_tensor(parts[:, 2, :], rest[:, :], parts[:, 1, :], ALU.subtract)\
                    .then_inc(lo, 1)

            def step(s, tail, back, body, head):
                t, u, n = s - 2, s - 1, s + 1
                if tail:
                    rstd_of(2, t)
                if head:
                    rstd_of(0, n)
                if back:
                    pool.wait_ge(x1_ready, u + 1)
                    if tail:
                        pool.wait_ge(x2_ready, t + 1)
                    nc.gpsimd.tensor_tensor(x1b[:, :, :], x1[:, :, :],
                                            out_bias[:, :].unsqueeze(1).to_broadcast([P, QB, D]), ALU.add)\
                        .then_inc(x1b_ready, 1)
                if tail:
                    pool.wait_ge(relu_ready, t + 1)
                    if later(t):
                        pool.wait_ge(fv_made, t)
                    nc.gpsimd.tensor_tensor(k_act[:, :, :], k_relu[:, :].rearrange("p (b t) -> p b t", b=QB),
                                            k_relu[:, :].rearrange("p (b t) -> p b t", b=QB), ALU.mult)\
                        .then_inc(k_act_ready, 1)
                if head:
                    low_part(k_parts, k_rest, k_left, k_mid, k_lo, k_stored, 96, n)
                if tail:
                    pool.wait_ge(y_gated_ready, t + 1)
                    if later(t):
                        pool.wait_ge(y_stored, 16 * t)
                    nc.gpsimd.tensor_tensor(y_out[:, :, :], y_gated[:, :].rearrange("p (b d) -> p b d", b=QB),
                                            x2[:, :, :], ALU.add).then_inc(y_ready, 1)
                if head:
                    low_part(q_parts, q_rest, q_left, q_mid, q_lo, q_stored, 32, n)
                    if not later(n):
                        nc.gpsimd.memset(cq_stack[:, :, :, :, :], 0.0).then_inc(cross_zeros, 1)
                        nc.gpsimd.memset(ck_stack[:, :, :, :], 1.0).then_inc(cross_zeros, 1)
                if body:
                    rstd_of(1, s)
                if body:
                    low_part(ck_parts, ck_rest, ck_left, ck_mid, ck_lo, ck_stored, 96, s)
                    low_part(cq_parts, cq_rest, cq_left, cq_mid, cq_lo, cq_stored, 32, s)

            pool.wait_ge(setup_dve, 8)
            schedule(pool, step)

        @block.scalar
        def _(act):
            act.wait_ge(w_turned, 2)
            for n in (CQ, CK, CV, CO, FR, FK, FV):
                src = proj[(n - CQ) // 4][:, P * ((n - CQ) % 4):P * ((n - CQ) % 4) + P]
                if n in (CQ, CK):
                    nc.scalar.activation(wT[:, n, :].rearrange("p (a d g) -> p a d g", a=2, d=DH),
                                         src.rearrange("p (g a d) -> p a d g", a=2, d=DH), ACT.Copy,
                                         scale=SCALE if n == CQ else 1.0).then_inc(w_ready, 1)
                else:
                    nc.scalar.activation(wT[:, n, :], src, ACT.Copy, scale=0.5 if n == FV else 1.0)\
                        .then_inc(w_ready, 1)

            def high_part(parts, src, made, stored, count, hi, q, bias=None):
                act.wait_ge(made, q + 1)
                if later(q):
                    act.wait_ge(stored, count * q)
                if bias is None:
                    nc.scalar.activation(parts[:, 0, :], src, ACT.Copy).then_inc(hi, 1)
                else:
                    nc.scalar.activation(parts[:, 0, :], src, ACT.Identity, bias=bias).then_inc(hi, 1)

            def mid_part(parts, rest, left, mid, q):
                act.wait_ge(left, q + 1)
                nc.scalar.activation(parts[:, 1, :], rest[:, :], ACT.Copy).then_inc(mid, 1)

            def step(s, tail, back, body, head):
                t, u, n = s - 2, s - 1, s + 1

                def exp_self(k):
                    act.wait_ge(sT_made, 8 * s + k + 1)
                    if k >= 3:
                        act.wait_ge(pv_done, 8 * s + k - 2)
                    elif later(s):
                        act.wait_ge(pv_done, 8 * s)
                    nc.scalar.activation(probs[:, k % 3].rearrange("p g a q -> p (g a q)"),
                                         score[ST_SLOT[k]][:, :], ACT.Exp).then_inc(exp_done, 1)

                def exp_cross(k):
                    act.wait_ge(csT_made, 8 * u + k + 1)
                    if k >= 2:
                        act.wait_ge(cpv_done, 8 * u + k - 1)
                    elif later(u):
                        act.wait_ge(cpv_done, 8 * u)
                    nc.scalar.activation(cprobs[0:TC, k % 2].rearrange("p g a q -> p (g a q)"),
                                         score[k % 2][0:TC, :], ACT.Exp).then_inc(cexp_done, 1)

                if body:
                    for k in range(4):
                        exp_self(k)
                if tail:
                    act.wait_ge(xeT_made, t + 1)
                    if later(t):
                        act.wait_ge(mix_ready, 2 * t)
                    for m in (1, 0):
                        nc.scalar.activation(mix_a[:, m, :, 1:T],
                                             proj[0][:, :].rearrange("p (b t) -> p b t", b=QB)[:, :, 0:T - 1],
                                             ACT.Identity, scale=mu_rest[:, m:m + 1]).then_inc(mix_part, 1)
                if body:
                    exp_self(4)
                if head:
                    act.wait_ge(xnT_made, n + 1)
                    if later(n):
                        act.wait_ge(v_made, n)
                    nc.scalar.activation(xnT[:, :], proj[1][:, :], ACT.Copy).then_inc(xnT_ready, 1)
                if body:
                    exp_self(5)
                if tail:
                    act.wait_ge(fk_made, t + 1)
                    if later(t):
                        act.wait_ge(k_act_ready, t)
                    nc.scalar.activation(k_relu[:, :], proj[0][:, :], ACT.Relu).then_inc(relu_ready, 1)
                if head:
                    high_part(k_parts, proj[1][:, :], k_made, k_stored, 96, k_hi, n)
                if body:
                    exp_self(6)
                if head:
                    mid_part(k_parts, k_rest, k_left, k_mid, n)
                if tail:
                    act.wait_ge(fr_made, t + 1)
                    if later(t):
                        act.wait_ge(y_gated_ready, t)
                    nc.scalar.activation(gate_tanh[:, :], proj[1][:, :], ACT.Tanh, scale=0.5)\
                        .then_inc(gate_tanh_ready, 1)
                if body:
                    exp_self(7)
                if back:
                    act.wait_ge(cmaxT_made, u + 1)
                    if later(u):
                        act.wait_ge(cmax_mid_ready, u)
                        act.wait_ge(cshift_in, 64 * u)
                    nc.scalar.activation(cmax_f[:, :], proj[0][0:2 * G * QB, 0:T], ACT.Copy)\
                        .then_inc(cmax_f_ready, 1)
                    act.wait_ge(cmax_f_ready, u + 1)
                    nc.scalar.activation(cmax_hi[:, :], cmax_f[:, :], ACT.Copy).then_inc(cmax_hi_ready, 1)
                if head:
                    high_part(q_parts, proj[1][:, :], q_made, q_stored, 32, q_hi, n)
                    mid_part(q_parts, q_rest, q_left, q_mid, n)
                if back:
                    exp_cross(0)
                if body:
                    act.wait_ge(ctxT_made, s + 1)
                    if later(s):
                        act.wait_ge(cv_made, s)
                    nc.scalar.activation(ctxT[:, :], proj[0][:, 0:NC], ACT.Copy).then_inc(ctxT_ready, 1)
                if back:
                    exp_cross(1)
                if head:
                    act.wait_ge(x_loaded, 16 * n + 16)
                    if body:
                        act.wait_ge(x1_ready, s + 1)
                    nc.scalar.activation(x_res[:, :, :], x_in[:, :, :], ACT.Copy).then_inc(x_kept, 1)
                if back:
                    exp_cross(2)
                if body:
                    high_part(ck_parts, proj[0][:, 0:NC], ck_made, ck_stored, 96, ck_hi, s, bias_cols[:, 1:2])
                    mid_part(ck_parts, ck_rest, ck_left, ck_mid, s)
                if back:
                    for k in range(3, 5):
                        exp_cross(k)
                if body:
                    act.wait_ge(xcT_made, s + 1)
                    if later(s):
                        act.wait_ge(cq_made, s)
                    nc.scalar.activation(xcT[:, :], proj[1][:, :], ACT.Copy).then_inc(xcT_ready, 1)
                if back:
                    exp_cross(5)
                    exp_cross(6)
                if head:
                    act.wait_ge(maxT_made, n + 1)
                    if later(n):
                        act.wait_ge(max_mid_ready, n)
                        act.wait_ge(shift_in, 64 * n)
                    for i in range(2):
                        nc.scalar.activation(max_f[:, :, HALF * i:HALF * i + HALF],
                                             proj[0][32 * i:32 * i + 32, 0:T]
                                             .rearrange("p (a q) -> p a q", a=2), ACT.Copy)\
                            .then_inc(max_f_ready, 1)
                    act.wait_ge(max_f_ready, 2 * n + 2)
                    nc.scalar.activation(max_hi[:, :, :], max_f[:, :, :], ACT.Copy).then_inc(max_hi_ready, 1)
                if body:
                    high_part(cq_parts, proj[1][:, :], cq_made, cq_stored, 32, cq_hi, s, bias_cols[:, 0:1])
                if back:
                    exp_cross(7)
                if body:
                    mid_part(cq_parts, cq_rest, cq_left, cq_mid, s)

            act.wait_ge(bias_ready, 3)
            act.wait_ge(pad_zeros, 4)
            schedule(act, step)

        @block.vector
        def _(dve):
            nc.vector.memset(head_ones[:, :, :], 0.0).then_inc(consts_made, 1)
            nc.vector.memset(one[:, :], 1.0).then_inc(consts_made, 1)
            nc.vector.memset(neg_half[:, :], -0.5).then_inc(consts_made, 1)
            nc.vector.memset(neg_max[:, :, :, :], 0.0).then_inc(consts_made, 1)
            nc.vector.memset(cneg_max[:, :, :, :], 0.0).then_inc(consts_made, 1)
            nc.vector.memset(q_stack[:, :, :, :, :], 0.0).then_inc(zeros_made, 1)
            dve.wait_ge(consts_made, 5)
            for i in range(4):
                nc.vector.memset(head_ones[:, i, DH * i:DH * i + DH], 1.0).then_inc(consts_made, 1)
            dve.wait_ge(ident_made, 3)
            for i in range(4):
                nc.vector.tensor_copy(ident_bf[:, i, :], ident[:, :]).then_inc(consts_made, 1)
            for s in range(2):
                nc.vector.tensor_copy(pick_lo[:, s, :], ident[:, 0:HALF]).then_inc(consts_made, 1)
                nc.vector.tensor_copy(pick_hi[:, s, :], ident[:, HALF:P]).then_inc(consts_made, 1)
            for s in range(2):
                nc.vector.tensor_copy(band_lo[:, 4 * s:4 * s + 4, :], band[:, :, 0:HALF]).then_inc(consts_made, 1)
            dve.wait_ge(w_in, 176)
            nc.vector.tensor_scalar(wT[:, SQ, :].rearrange("p (a d g) -> p a d g", a=2, d=DH),
                                    w_raw[:, SQ, :].rearrange("p (g a d) -> p a d g", a=2, d=DH),
                                    SCALE, None, ALU.mult).then_inc(w_ready, 1)
            nc.vector.tensor_copy(wT[:, SK, :].rearrange("p (a d g) -> p a d g", a=2, d=DH),
                                  w_raw[:, SK, :].rearrange("p (g a d) -> p a d g", a=2, d=DH)).then_inc(w_ready, 1)
            nc.vector.tensor_copy(wT[:, SV, :], w_raw[:, SV, :]).then_inc(w_ready, 1)
            nc.vector.tensor_copy(wT[:, SO, :], w_raw[:, SO, :]).then_inc(w_ready, 1)
            dve.wait_ge(small_in, 96)
            nc.vector.tensor_scalar(bias_perm[:, 0, :].rearrange("p (a d g) -> p a d g", a=2, d=DH),
                                    bias_rows[:, 0, :].rearrange("p (g a d) -> p a d g", a=2, d=DH),
                                    SCALE, None, ALU.mult).then_inc(bias_permuted, 1)
            nc.vector.tensor_copy(bias_perm[:, 1, :].rearrange("p (a d g) -> p a d g", a=2, d=DH),
                                  bias_rows[:, 1, :].rearrange("p (g a d) -> p a d g", a=2, d=DH))\
                .then_inc(bias_permuted, 1)
            nc.vector.tensor_copy(bias_perm[:, 2, :], bias_rows[:, 2, :]).then_inc(bias_permuted, 1)
            nc.vector.tensor_scalar(mu_rest[:, :], mu[:, :], -1.0, 1.0, ALU.mult, ALU.add).then_inc(setup_dve, 1)
            dve.wait_ge(bias_turned, 3)
            nc.vector.tensor_copy(bias_cols[:, :], score[0][:, 0:3]).then_inc(bias_ready, 3)
            dve.wait_ge(bias_ready, 3)
            nc.vector.tensor_scalar(cbv_wide[:, :], one[:, :], bias_cols[:, 2:3], None, ALU.mult)\
                .then_inc(bias_wide, 1)
            dve.wait_ge(out_bias_mm, 1)
            nc.vector.tensor_tensor(out_bias[:, :], score[0][:, 0:P], cbo_wide[:, :], ALU.add).then_inc(setup_dve, 7)
            def split_mask():
                dve.wait_ge(mask_loaded, 16)
                nc.vector.tensor_scalar(mask_f[:, :], mask_in[:, :], MASK_WEIGHT, None, ALU.mult)\
                    .then_inc(bias_permuted, 1)
                dve.wait_ge(bias_permuted, 4)
                nc.vector.tensor_copy(mask_parts[:, 0, :], mask_f[:, :]).then_inc(bias_permuted, 1)
                dve.wait_ge(bias_permuted, 5)
                nc.vector.tensor_tensor(mask_r[:, :], mask_f[:, :], mask_parts[:, 0, :], ALU.subtract)\
                    .then_inc(bias_permuted, 1)
                dve.wait_ge(bias_permuted, 6)
                nc.vector.tensor_copy(mask_parts[:, 1, :], mask_r[:, :]).then_inc(setup_dve, 1)
                dve.wait_ge(setup_dve, 9)
                nc.vector.tensor_tensor(mask_parts[:, 2, :], mask_r[:, :], mask_parts[:, 1, :], ALU.subtract)\
                    .then_inc(setup_dve, 1)

            def moments_of(n, src, q):
                for b in range(QB):
                    nc.vector.bn_stats(stats[n][:, b, :], src[:, b, :]).then_inc(ln_stats[n], 1)
                dve.wait_ge(ln_stats[n], QB * q + QB)
                if later(q):
                    dve.wait_ge(ln_rstd[n], q)
                mo, st = moments[n], stats[n]
                nc.vector.tensor_tensor(mo[:, 0], st[:, :, 1], st[:, :, 4], ALU.add).then_inc(ln_moments[n], 1)
                nc.vector.tensor_tensor(mo[:, 1], st[:, :, 1], st[:, :, 4], ALU.subtract).then_inc(ln_moments[n], 1)
                nc.vector.tensor_tensor(mo[:, 2], st[:, :, 2], st[:, :, 5], ALU.add).then_inc(ln_moments[n], 1)
                dve.wait_ge(ln_moments[n], 7 * q + 3)
                nc.vector.tensor_scalar(mo[:, 3], mo[:, 0], 0.5, None, ALU.mult).then_inc(ln_moments[n], 1)
                nc.vector.scalar_tensor_tensor(out=mo[:, 4], in0=mo[:, 1], scalar=0.25, in1=mo[:, 1],
                                               op0=ALU.mult, op1=ALU.mult).then_inc(ln_moments[n], 1)
                nc.vector.tensor_scalar(mo[:, 5], mo[:, 2], 1.0 / D, EPS, ALU.mult, ALU.add)\
                    .then_inc(ln_moments[n], 1)
                dve.wait_ge(ln_moments[n], 7 * q + 6)
                nc.vector.tensor_tensor(var_eps[n][:, :], mo[:, 4], mo[:, 5], ALU.add).then_inc(ln_moments[n], 1)

            def norm_of(n, src, q, turned):
                dve.wait_ge(ln_rstd[n], q + 1)
                if later(q):
                    dve.wait_ge(turned, q)
                for b in range(QB):
                    nc.vector.tensor_scalar(xn[n][:, b, :], src[:, b, :], moments[n][:, 3, b:b + 1],
                                            rstd[n][:, b:b + 1], ALU.subtract, ALU.mult).then_inc(ln_out[n], 1)

            def rest_of(src, parts, rest, hi, lo, left, q, bias=None):
                dve.wait_ge(hi, q + 1)
                if later(q):
                    dve.wait_ge(lo, q)
                if bias is None:
                    nc.vector.tensor_tensor(rest[:, :], src, parts[:, 0, :], ALU.subtract).then_inc(left, 1)
                else:
                    nc.vector.scalar_tensor_tensor(out=rest[:, :], in0=src, scalar=bias, in1=parts[:, 0, :],
                                                   op0=ALU.add, op1=ALU.subtract).then_inc(left, 1)

            def spread(values, src, rows, made, pv, ready, q):
                dve.wait_ge(made, q + 1)
                if later(q):
                    dve.wait_ge(pv, 8 * q)
                for b in range(QB):
                    nc.vector.tensor_copy(v_diag(values, b, rows),
                                          src[0:rows, D * b:D * b + D].rearrange("p (g i d) -> p g i d", i=4, d=DH))\
                        .then_inc(ready, 1)

            def normalize(b, q, pv, inv, inv_ready, att, ready, used):
                dve.wait_ge(pv, 8 * q + 2 * b + 2)
                if b >= 2:
                    dve.wait_ge(ready, 4 * q + b - 1)
                elif later(q):
                    dve.wait_ge(ready, 4 * q)
                nc.vector.reciprocal(inv[:, b % 2, :], sums[b % 2][:, 1, :]).then_inc(inv_ready, 1)
                dve.wait_ge(inv_ready, 4 * q + b + 1)
                if later(q) and b == 0:
                    dve.wait_ge(used, q)
                nc.vector.tensor_tensor(att[:, b, :], sums[b % 2][:, 0, :], inv[:, b % 2, :], ALU.mult)\
                    .then_inc(ready, 1)

            def step(s, tail, back, body, head):
                t, u, n = s - 2, s - 1, s + 1

                def max_self(k):
                    dve.wait_ge(s_made, 6 * n + k + 1)
                    if k == 0 and later(n):
                        dve.wait_ge(maxT_made, n)
                    bb, kind = 2 * (k // 3), k % 3
                    if kind < 2:
                        nc.vector.tensor_reduce(neg_max[:, 1, :, bb + kind],
                                                score[k % 2][:, :].rearrange("p (g k) -> p g k", g=G),
                                                AX_X, ALU.max, negate=True).then_inc(max_taken, 1)
                    else:
                        nc.vector.tensor_reduce(neg_max[:, 0, :, bb:bb + 2].rearrange("p g b -> p b g"),
                                                score[k % 2][:, :].rearrange("p (b g k) -> p b g k", b=2, g=G),
                                                AX_X, ALU.max, negate=True).then_inc(max_taken, 1)

                def max_cross(k):
                    b, a = k // 2, k % 2
                    dve.wait_ge(cs_made, 8 * u + k + 1)
                    if k == 0 and later(u):
                        dve.wait_ge(cmaxT_made, u)
                    src = score[MC_SLOT[k]][:, :].rearrange("p (n c) -> p n c", n=2)[:, :, 0:4 * TC]\
                        .rearrange("p n (i k) -> p n i k", k=TC)
                    nc.vector.tensor_reduce(cneg_max[:, a, :, b].rearrange("p (n i) -> p n i", n=2), src,
                                            AX_X, ALU.max, negate=True).then_inc(cmax_taken, 1)

                def normalize_self(b):
                    normalize(b, s, pv_done, den_inv, den_ready, attT, att_ready, o_made)

                def normalize_cross(b):
                    normalize(b, u, cpv_done, cden_inv, cden_ready, cattT, catt_ready, co_made)

                if tail:
                    dve.wait_ge(co_made, t + 1)
                    dve.wait_ge(x1b_ready, t + 1)
                    if later(t):
                        dve.wait_ge(y_ready, t)
                        dve.wait_ge(ln_out[2], QB * t)
                    nc.vector.tensor_tensor(x2[:, :, :], proj[1][:, :].rearrange("p (b d) -> p b d", b=QB),
                                            x1b[:, :, :], ALU.add).then_inc(x2_ready, 1)
                    dve.wait_ge(x2_ready, t + 1)
                    moments_of(2, x2, t)
                if head:
                    dve.wait_ge(x_loaded, 16 * n + 16)
                    moments_of(0, x_in, n)
                if tail:
                    norm_of(2, x2, t, xeT_made)
                if head:
                    norm_of(0, x_in, n, xnT_made)
                if body:
                    normalize_self(0)
                if back:
                    max_cross(0)
                if tail:
                    dve.wait_ge(mix_part, 2 * t + 2)
                    if later(t):
                        dve.wait_ge(fk_made, t)
                        dve.wait_ge(fr_made, t)
                    for m in (1, 0):
                        nc.vector.scalar_tensor_tensor(out=mixed[:, m],
                                                       in0=proj[0][:, :].rearrange("p (b t) -> p b t", b=QB),
                                                       scalar=mu[:, m:m + 1], in1=mix_a[:, m],
                                                       op0=ALU.mult, op1=ALU.add).then_inc(mix_ready, 1)
                if back:
                    max_cross(1)
                if body:
                    normalize_self(1)
                if back:
                    max_cross(2)
                    max_cross(3)
                if head:
                    rest_of(proj[1][:, :], k_parts, k_rest, k_hi, k_lo, k_left, n)
                if back:
                    max_cross(4)
                    max_cross(5)
                if body:
                    normalize_self(2)
                if back:
                    max_cross(6)
                if tail:
                    dve.wait_ge(gate_tanh_ready, t + 1)
                    dve.wait_ge(fv_made, t + 1)
                    if later(t):
                        dve.wait_ge(y_ready, t)
                    nc.vector.scalar_tensor_tensor(out=y_gated[:, :], in0=gate_tanh[:, :], scalar=1.0,
                                                   in1=proj[0][:, :], op0=ALU.add, op1=ALU.mult)\
                        .then_inc(y_gated_ready, 1)
                if back:
                    max_cross(7)
                if back:
                    dve.wait_ge(cmax_hi_ready, u + 1)
                    nc.vector.tensor_tensor(cmax_mid[:, :], cmax_f[:, :], cmax_hi[:, :], ALU.subtract)\
                        .then_inc(cmax_mid_ready, 1)
                if head:
                    rest_of(proj[1][:, :], q_parts, q_rest, q_hi, q_lo, q_left, n)
                if body:
                    normalize_self(3)
                if body:
                    dve.wait_ge(o_made, s + 1)
                    if later(s):
                        dve.wait_ge(x1b_ready, s)
                        dve.wait_ge(ln_out[1], QB * s)
                    dve.wait_ge(x_kept, s + 1)
                    nc.vector.tensor_tensor(x1[:, :, :], proj[1][:, :].rearrange("p (b d) -> p b d", b=QB),
                                            x_res[:, :, :], ALU.add).then_inc(x1_ready, 1)
                if head:
                    spread(v_heads, proj[0], P, v_made, pv_done, v_ready, n)
                if body:
                    dve.wait_ge(x1_ready, s + 1)
                    moments_of(1, x1, s)
                    rest_of(proj[0][:, 0:NC], ck_parts, ck_rest, ck_hi, ck_lo, ck_left, s, bias_cols[:, 1:2])
                    norm_of(1, x1, s, xcT_made)
                if head and not later(n):
                    split_mask()
                if back:
                    normalize_cross(0)
                    normalize_cross(1)
                if head:
                    for k in range(6):
                        max_self(k)
                if head:
                    dve.wait_ge(max_hi_ready, n + 1)
                    nc.vector.tensor_tensor(max_mid[:, :, :], max_f[:, :, :], max_hi[:, :, :], ALU.subtract)\
                        .then_inc(max_mid_ready, 1)
                if body:
                    rest_of(proj[1][:, :], cq_parts, cq_rest, cq_hi, cq_lo, cq_left, s, bias_cols[:, 0:1])
                if back:
                    normalize_cross(2)
                    normalize_cross(3)
                if body:
                    spread(cv_heads, proj[0], TC, cv_made, cpv_done, cv_ready, s)

            def v_diag(heads, b, rows):
                flat = heads[0:rows, b].rearrange("p (g i) c -> p g (i c)", i=4)
                skew = bass.AP(tensor=flat.tensor, offset=flat.offset,
                               ap=[list(flat.ap[0]), [128, 4], [40, 4], [1, DH]])
                return skew

            dve.wait_ge(pad_zeros, 4)
            schedule(dve, step)

        @block.tensor
        def _(pe):
            pe.wait_ge(ident_made, 1)
            pe.wait_ge(w_in, 176)
            for n in (CQ, CK, CV, CO, FR, FK, FV):
                j = n - CQ
                last = nc.tensor.transpose(proj[j // 4][:, P * (j % 4):P * (j % 4) + P], w_raw[:, n, :], ident[:, :])
                if n in (CO, FV):
                    last.then_inc(w_turned, 1)
            pe.wait_ge(bias_permuted, 3)
            pe.wait_ge(consts_made, 5)
            for n in range(3):
                nc.tensor.matmul(score[0][:, n:n + 1], bias_perm[0:1, n, :], one[0:1, 0:1], start=True, stop=True)\
                    .then_inc(bias_turned, 1)
            pe.wait_ge(bias_wide, 1)
            pe.wait_ge(w_ready, 11)
            nc.tensor.matmul(score[0][:, 0:P], cbv_wide[:, :], wT[:, CO, :], start=True, stop=True)\
                .then_inc(out_bias_mm, 1)
            pe.wait_ge(consts_made, 19)
            pe.wait_ge(setup_dve, 8)

            def turn(dst, src, rows):
                for b in range(QB):
                    last = nc.tensor.transpose(dst[:, rows * b:rows * b + rows], src[0:rows, b, :],
                                               ident[0:rows, 0:rows])
                return last

            def score_max_self(k):
                bb, kind = 2 * (k // 3), k % 3
                dst = score[k % 2]
                if kind < 2:
                    b = bb + kind
                    for n in range(2):
                        nc.tensor.matmul(dst[:, 512 * n:512 * n + 512], pick_hi[:, :, :], band[:, :, :],
                                         start=True, stop=False)
                    for g in range(G):
                        for a in range(2):
                            last = nc.tensor.matmul(dst[HALF * a:HALF * a + HALF, T * g:T * g + T],
                                                    q_stack[0:NSTACK, a, g, b, HALF:T],
                                                    k_stack[0:NSTACK, g, b, :], start=False, stop=(g % 4 == 3))
                else:
                    for n in range(2):
                        nc.tensor.matmul(dst[:, 512 * n:512 * n + 512], pick_lo[:, :, :], band_lo[:, :, :],
                                         start=True, stop=False)
                        for g in range(G):
                            c = 512 * n + HALF * g
                            for a in range(2):
                                last = nc.tensor.matmul(dst[HALF * a:HALF * a + HALF, c:c + HALF],
                                                        q_stack[0:NSTACK, a, g, bb + n, 0:HALF],
                                                        k_stack[0:NSTACK, g, bb + n, 0:HALF],
                                                        start=False, stop=(g == G - 1))
                last.then_inc(s_made, 1)

            def attend(k, probs_in, values, ready, ready_value, done):
                b, j = k // 2, k % 2
                pe.wait_ge(ready, ready_value)
                dst = sums[b % 2]
                for a in range(2):
                    for g in range(4):
                        nc.tensor.matmul(dst[32 * g:32 * g + 32, 0, :], values[:, b, 4 * g + 2 * j + a, :],
                                         probs_in[:, g, a, :], start=(j == 0 and a == 0),
                                         stop=(j == 1 and a == 1), tile_position=(0, 32 * g),
                                         skip_group_check=True)
                for a in range(2):
                    for g in range(4):
                        last = nc.tensor.matmul(dst[32 * g:32 * g + 32, 1, :], head_ones[:, 2 * j + a, :],
                                                probs_in[:, g, a, :], start=False,
                                                stop=(j == 1 and a == 1), tile_position=(0, 32 * g),
                                                skip_group_check=True)
                last.then_inc(done, 1)

            def project_out(att, w, ready, q, dst, made):
                for b in range(QB):
                    pe.wait_ge(ready, QB * q + b + 1)
                    last = nc.tensor.matmul(dst[:, D * b:D * b + D], att[:, b, :], wT[:, w, :],
                                            start=True, stop=True)
                last.then_inc(made, 1)

            def step(s, tail, back, body, head):
                t, u, n = s - 2, s - 1, s + 1

                def self_slot(k):
                    if k == 0:
                        pe.wait_ge(q_stacked, 96 * n + 96)
                        pe.wait_ge(k_stacked, 32 * n + 32)
                    if k >= 2:
                        pe.wait_ge(max_taken, 6 * n + k - 1)
                    elif k == 1 and back:
                        pe.wait_ge(cexp_done, 8 * u + 6)
                    score_max_self(k)

                def cross_slot(k):
                    b, a = k // 2, k % 2
                    if k == 0:
                        pe.wait_ge(cq_stacked, 96 * u + 96)
                        pe.wait_ge(ck_stacked, 32 * u + 32)
                        pe.wait_ge(cbias_in, 16 * u + 16)
                        if body:
                            pe.wait_ge(exp_done, 8 * s + 4)
                    else:
                        pe.wait_ge(cmax_taken, 8 * u + k)
                    if k == 7 and body:
                        pe.wait_ge(exp_done, 8 * s + 8)
                    dst = score[MC_SLOT[k]]
                    for g in range(G):
                        c = 512 * (g // 4) + TC * (g % 4)
                        last = nc.tensor.matmul(dst[:, c:c + TC], cq_stack[0:SHIFT_CROSS, a, g, b, :],
                                                ck_stack[0:SHIFT_CROSS, g, b, :], start=True, stop=True)
                    last.then_inc(cs_made, 1)

                def self_scores(k):
                    b, j = k // 2, k % 2
                    dst = score[ST_SLOT[k]]
                    if 2 <= k < 5:
                        pe.wait_ge(exp_done, 8 * s + k - 1)
                    elif k >= 5:
                        pe.wait_ge(exp_done, 8 * s + k)
                    for m in range(2):
                        nc.tensor.matmul(dst[:, 512 * m:512 * m + 512], band[:, 0, :], ident_bf[:, :, :],
                                         start=True, stop=False)
                    for i in range(4):
                        g = 2 * i + j
                        last = nc.tensor.matmul(dst[:, 256 * i:256 * i + 256], k_stack[:, g, b, :],
                                                q_stack[:, :, g, b, :], start=False, stop=(i % 2 == 1))
                    last.then_inc(sT_made, 1)

                def attend_self(k):
                    if k >= 4 and k % 2 == 0:
                        pe.wait_ge(att_ready, 4 * s + k // 2 - 1)
                    attend(k, probs[:, k % 3], v_heads, exp_done, 8 * s + k + 1, pv_done)

                def cross_scores(k):
                    b, j = k // 2, k % 2
                    if 2 <= k < 6:
                        pe.wait_ge(cexp_done, 8 * u + k - 1)
                    elif k >= 6 and head:
                        pe.wait_ge(max_taken, 6 * n + k - 1)
                    elif k >= 6:
                        pe.wait_ge(cexp_done, 8 * u + k - 1)
                    for i in range(4):
                        g = 2 * i + j
                        last = nc.tensor.matmul(score[k % 2][0:TC, 256 * i:256 * i + 256], ck_stack[:, g, b, :],
                                                cq_stack[:, :, g, b, :], start=True, stop=True)
                    last.then_inc(csT_made, 1)

                def attend_cross(k):
                    if k >= 4 and k % 2 == 0:
                        pe.wait_ge(catt_ready, 4 * u + k // 2 - 1)
                    attend(k, cprobs[:, k % 2], cv_heads, cexp_done, 8 * u + k + 1, cpv_done)

                def mix_turn():
                    pe.wait_ge(ln_out[2], QB * t + QB)
                    if back:
                        pe.wait_ge(cv_ready, QB * s)
                    else:
                        pe.wait_ge(y_gated_ready, t)
                    turn(proj[0], xn[2], T).then_inc(xeT_made, 1)

                def mix_key():
                    pe.wait_ge(mix_ready, 2 * t + 2)
                    nc.tensor.matmul(proj[0][:, :], wT[:, FK, :], mixed[:, 1].rearrange("p b t -> p (b t)"),
                                     start=True, stop=True).then_inc(fk_made, 1)

                def mix_gate():
                    pe.wait_ge(x2_ready, t + 1)
                    if head:
                        pe.wait_ge(k_left, n + 1)
                    for b in range(QB):
                        last = nc.tensor.matmul(proj[1][:, D * b:D * b + D], mixed[:, 0, b, :], wT[:, FR, :],
                                                start=True, stop=True)
                    last.then_inc(fr_made, 1)

                def mix_value():
                    pe.wait_ge(relu_ready, t + 1)
                    pe.wait_ge(k_act_ready, t + 1)
                    for b in range(QB):
                        last = nc.tensor.matmul(proj[0][:, D * b:D * b + D], k_act[:, b, :], wT[:, FV, :],
                                                start=True, stop=True)
                    last.then_inc(fv_made, 1)

                if tail:
                    if back:
                        pe.wait_ge(cq_left, s)
                    else:
                        pe.wait_ge(gate_tanh_ready, t)
                    project_out(cattT, CO, catt_ready, t, proj[1], co_made)
                if body:
                    pe.wait_ge(shift_in, 64 * s + 64)
                    self_scores(0)
                    self_scores(1)
                    self_scores(2)
                    attend_self(0)
                    self_scores(3)
                    attend_self(1)
                if tail:
                    mix_turn()
                if body:
                    self_scores(4)
                    attend_self(2)
                if head:
                    pe.wait_ge(ln_out[0], QB * n + QB)
                    if tail:
                        pe.wait_ge(x2_ready, t + 1)
                    elif back:
                        pe.wait_ge(cq_left, s)
                    elif body:
                        pe.wait_ge(q_left, n)
                    turn(proj[1], xn[0], T).then_inc(xnT_made, 1)
                if back:
                    cross_slot(0)
                if body:
                    self_scores(5)
                if back:
                    cross_slot(1)
                if body:
                    attend_self(3)
                if tail:
                    mix_key()
                if head:
                    pe.wait_ge(xnT_ready, n + 1)
                    nc.tensor.matmul(proj[1][:, :], wT[:, SK, :], xnT[:, :], start=True, stop=True)\
                        .then_inc(k_made, 1)
                if back:
                    cross_slot(2)
                if body:
                    self_scores(6)
                if back:
                    cross_slot(3)
                if body:
                    attend_self(4)
                if back:
                    cross_slot(4)
                if body:
                    self_scores(7)
                if back:
                    cross_slot(5)
                if body:
                    attend_self(5)
                if tail:
                    mix_gate()
                if back:
                    cross_slot(6)
                if tail:
                    mix_value()
                if back:
                    cross_slot(7)
                if body:
                    attend_self(6)
                if back:
                    pe.wait_ge(cmax_taken, 8 * u + 8)
                    if tail:
                        pe.wait_ge(y_gated_ready, t + 1)
                    else:
                        pe.wait_ge(cv_ready, QB * s)
                    nc.tensor.transpose(proj[0][:, 0:T], cneg_max[:, :, :, :], ident[:, :]).then_inc(cmaxT_made, 1)
                if head:
                    if tail:
                        pe.wait_ge(gate_tanh_ready, t + 1)
                    pe.wait_ge(k_left, n + 1)
                    nc.tensor.matmul(proj[1][:, :], wT[:, SQ, :], xnT[:, :], start=True, stop=True)\
                        .then_inc(q_made, 1)
                if body:
                    attend_self(7)
                if body:
                    if head:
                        pe.wait_ge(q_left, n + 1)
                    elif tail:
                        pe.wait_ge(gate_tanh_ready, t + 1)
                    project_out(attT, SO, att_ready, s, proj[1], o_made)
                if head:
                    if back:
                        pe.wait_ge(cmax_f_ready, u + 1)
                    elif body:
                        pe.wait_ge(max_f_ready, 2)
                    for b in range(QB):
                        last = nc.tensor.matmul(proj[0][:, D * b:D * b + D], xnT[:, T * b:T * b + T], wT[:, SV, :],
                                                start=True, stop=True)
                    last.then_inc(v_made, 1)
                if back:
                    pe.wait_ge(cshift_in, 64 * u + 64)
                    pe.wait_ge(cv_ready, QB * u + QB)
                    cross_scores(0)
                    cross_scores(1)
                if body:
                    pe.wait_ge(ctx_loaded, 16 * s + 16)
                    if head:
                        pe.wait_ge(v_ready, QB * n + QB)
                    else:
                        pe.wait_ge(cmax_f_ready, u + 1)
                    turn(proj[0], ctx_in, TC).then_inc(ctxT_made, 1)
                if back:
                    attend_cross(0)
                    cross_scores(2)
                if body:
                    pe.wait_ge(ctxT_ready, s + 1)
                    nc.tensor.matmul(proj[0][:, 0:NC], wT[:, CK, :], ctxT[:, :], start=True, stop=True)\
                        .then_inc(ck_made, 1)
                if back:
                    attend_cross(1)
                    cross_scores(3)
                    attend_cross(2)
                    cross_scores(4)
                    attend_cross(3)
                if body:
                    pe.wait_ge(ln_out[1], QB * s + QB)
                    pe.wait_ge(x1_ready, s + 1)
                    turn(proj[1], xn[1], T).then_inc(xcT_made, 1)
                if back:
                    cross_scores(5)
                    attend_cross(4)
                if head:
                    for k in range(6):
                        self_slot(k)
                if back:
                    cross_scores(6)
                if body:
                    pe.wait_ge(xcT_ready, s + 1)
                    nc.tensor.matmul(proj[1][:, :], wT[:, CQ, :], xcT[:, :], start=True, stop=True)\
                        .then_inc(cq_made, 1)
                if head:
                    pe.wait_ge(max_taken, 6 * n + 6)
                    if body:
                        pe.wait_ge(ck_left, s + 1)
                    else:
                        pe.wait_ge(v_ready, QB)
                    nc.tensor.transpose(proj[0][:, 0:T], neg_max[:, :, :, :], ident[:, :]).then_inc(maxT_made, 1)
                if back:
                    cross_scores(7)
                    attend_cross(5)
                    attend_cross(6)
                    attend_cross(7)
                if body:
                    pe.wait_ge(ck_left, s + 1)
                    if head:
                        pe.wait_ge(max_f_ready, 2 * n + 2)
                    for b in range(QB):
                        last = nc.tensor.matmul(proj[0][0:TC, D * b:D * b + D], ctxT[:, TC * b:TC * b + TC],
                                                wT[:, CV, :], start=True, stop=True)
                    last.then_inc(cv_made, 1)

            schedule(pe, step)


_INS = ['x', 'ctx_1024', 'mask_BxS2_ik1', 'L0_attn_Wq', 'L0_attn_Wk', 'L0_attn_Wv', 'L0_attn_Wo',
        'L0_xattn_Wq', 'L0_xattn_bq', 'L0_xattn_Wk', 'L0_xattn_bk', 'L0_xattn_Wv', 'L0_xattn_bv',
        'L0_xattn_Wo', 'L0_xattn_bo', 'L0_ffn_W_r', 'L0_ffn_W_k', 'L0_ffn_W_v', 'L0_ffn_mu_r', 'L0_ffn_mu_k']
_OUTS = [((BATCH, T, D), 'float32')]


def kernel(**inputs):
    import numpy as _np
    import concourse.bacc as _bacc
    from concourse import mybir as _mybir
    from concourse.bass_utils import run_bass_kernel_spmd as _run

    nc = _bacc.Bacc("TRN2", target_bir_lowering=False, num_devices=1)
    arrays, args = {}, []
    for name in _INS:
        a = _np.ascontiguousarray(inputs[name])
        arrays[f"in_{name}_dram"] = a
        args.append(nc.dram_tensor(f"in_{name}_dram", a.shape, _mybir.dt.from_np(a.dtype), kind="ExternalInput").ap())
    for i, (shape, dtype) in enumerate(_OUTS):
        dt = _mybir.dt.from_np(_np.dtype(dtype))
        args.append(nc.dram_tensor(f"out_{i}_dram", shape, dt, kind="ExternalOutput").ap())
    decoder_layer(nc, *args)
    r = _run(nc, [arrays], core_ids=[0])
    got = tuple(r.results[0][f"out_{i}_dram"] for i in range(len(_OUTS)))
    return got[0]
```
